# Optimizing a Trainium2 kernel written in Bass

```python
import numpy as np
import jax
import jax.numpy as jnp

def _softmax(x, axis=-1):
    return jax.nn.softmax(x, axis=axis)

def _gelu(x):
    return jax.nn.gelu(x, approximate=True)

def _silu(x):
    return jax.nn.silu(x)

def _sigmoid(x):
    return jax.nn.sigmoid(x)

def _layernorm(x, axis=-1, eps=1e-05):
    m = jnp.mean(x, axis=axis, keepdims=True)
    v = jnp.var(x, axis=axis, keepdims=True)
    return (x - m) / jnp.sqrt(v + eps)

def _scatter_add(tgt, idx, src, axis=0):
    return tgt.at[idx].add(src)

def _segment_sum(src, seg, n):
    return jax.ops.segment_sum(src, seg, n)
kernel_name = 'mk_decoder_preln_d1_seqx_r8_3924ef'

def setup_inputs(seed: int=0):
    np.random.seed(seed)
    _w = jnp.asarray

    def _rec_inputs():
        import jax
        import jax.numpy as jnp
        _rk = jax.random.key(seed)
        x = -0.0002928 + 1 * jax.random.normal(jax.random.fold_in(_rk, 1), (8, 128, 128), jnp.float32)
        _lenS = 128 - jax.random.randint(jax.random.fold_in(_rk, 7), (8,), 0, max(1, 128 // 4) + 1, jnp.int32)
        _lenS2 = 120 - jax.random.randint(jax.random.fold_in(_rk, 8), (8,), 0, max(1, 120 // 4) + 1, jnp.int32)
        _ctx_1024P = jax.random.normal(jax.random.fold_in(_rk, 11), (8, 16, 128), jnp.float32)
        _ctx_1024c = jax.random.dirichlet(jax.random.fold_in(_rk, 511), 0.3 * jnp.ones((16,), jnp.float32), (8, 120))
        _ctx_1024t = jnp.einsum('bsk,bkd->bsd', _ctx_1024c, _ctx_1024P)
        _ctx_1024t = _ctx_1024t * jax.lax.rsqrt(jnp.mean(jnp.square(_ctx_1024t)) + 1e-12) * 0.953939
        ctx_1024 = -1.39393e-06 + 0.999914 * (_ctx_1024t + 0.3 * jax.random.normal(jax.random.fold_in(_rk, 611), (8, 120, 128), jnp.float32))
        _validS = jnp.arange(128)[None, :] < _lenS[:, None]
        _validS2 = jnp.arange(120)[None, :] < _lenS2[:, None]
        _causal = jnp.tril(jnp.ones((128, 128), dtype=bool))
        mask_BxSxS2_bf0 = jnp.logical_not(jnp.ones((8, 128, 120), dtype=bool))
        return (x, ctx_1024, mask_BxSxS2_bf0)
    x, ctx_1024, mask_BxSxS2_bf0 = _rec_inputs()

    def _L0_attn_setup():
        import jax, jax.numpy as jnp
        import numpy as np
        from jax import lax
        B, T, HID, NH = (4, 256, 128, 16)
        D = HID // NH
        LN_EPS = 1e-05
        NORM_EPS = 1e-06
        key = jax.random.key(seed)
        ks = jax.random.split(key, 3)
        s = 0.02
        return {'x': jax.random.normal(ks[0], (B, T, HID), jnp.float32), 'ln_g': jnp.ones((HID,), jnp.float32), 'ln_b': jnp.zeros((HID,), jnp.float32), 'w_qkvb': jax.random.normal(ks[1], (HID, 4 * HID), jnp.float32) * s, 'b_qkvb': jnp.zeros((4 * HID,), jnp.float32), 'w_out': jax.random.normal(ks[2], (HID, HID), jnp.float32) * s, 'b_out': jnp.zeros((HID,), jnp.float32)}
    _L0_attn_all = _L0_attn_setup()
    _L0_attn_in = {k: v for k, v in _L0_attn_all.items() if k in ('ln_g', 'ln_b', 'w_qkvb', 'b_qkvb', 'w_out', 'b_out')}
    del _L0_attn_all

    def _L0_xattn_setup():
        import jax, jax.numpy as jnp
        import numpy as np
        D_MODEL = 128
        N_HEADS = 16
        D_K = 64
        D_V = 64
        INIT_RANGE = 0.1
        INF = 1000000000.0
        B, L = (8, 64)

        def _pos_emb(pos):
            d = D_MODEL
            freq = 1.0 / 10000.0 ** (jnp.arange(0, d, 2, dtype=jnp.float32) / d)
            ang = pos[:, None] * freq[None, :]
            scale = INIT_RANGE * d
            emb = jnp.stack([jnp.sin(ang) * scale, jnp.cos(ang) * scale], axis=-1)
            return emb.reshape(pos.shape[0], d)
        key = jax.random.key(seed)
        ks = jax.random.split(key, 13)
        u = lambda k, shape: jax.random.uniform(k, shape, jnp.float32, -INIT_RANGE, INIT_RANGE)
        return {'q': jax.random.normal(ks[0], (B, L, D_MODEL), jnp.float32), 'k': jax.random.normal(ks[1], (B, L, D_MODEL), jnp.float32), 'v': jax.random.normal(ks[2], (B, L, D_MODEL), jnp.float32), 'attn_mask': jnp.zeros((B, L, L), bool), 'Wq': u(ks[3], (D_MODEL, N_HEADS * D_K)), 'Wk': u(ks[4], (D_MODEL, N_HEADS * D_K)), 'Wv': u(ks[5], (D_MODEL, N_HEADS * D_V)), 'Wr': u(ks[6], (D_MODEL, N_HEADS * D_V)), 'ub_w': u(ks[7], (D_K,)), 'vb_w': u(ks[8], (D_K,)), 'head_w': u(ks[9], (D_MODEL, N_HEADS)), 'Wo': u(ks[10], (N_HEADS * D_V, D_MODEL)), 'ln_g': jnp.ones((D_MODEL,), jnp.float32), 'ln_b': jnp.zeros((D_MODEL,), jnp.float32)}
    _L0_xattn_all = _L0_xattn_setup()
    _L0_xattn_in = {k: v for k, v in _L0_xattn_all.items() if k in ('Wq', 'Wk', 'Wv', 'Wr', 'ub_w', 'vb_w', 'head_w', 'Wo', 'ln_g', 'ln_b')}
    del _L0_xattn_all

    def _L0_ffn_setup():
        import jax, jax.numpy as jnp
        import numpy as np
        B, T, C = (4, 256, 128)
        E = 8
        K = 2
        H = 176
        HS = 176 * 2
        key = jax.random.key(seed)
        k = jax.random.split(key, 8)
        s = 0.02
        return {'x': jax.random.normal(k[0], (B, T, C), jnp.float32), 'Wg': jax.random.normal(k[1], (C, E), jnp.float32) * s, 'W1': jax.random.normal(k[2], (E, C, H), jnp.float32) * s, 'W2': jax.random.normal(k[3], (E, C, H), jnp.float32) * s, 'W3': jax.random.normal(k[4], (E, H, C), jnp.float32) * s, 'Ws1': jax.random.normal(k[5], (C, HS), jnp.float32) * s, 'Ws2': jax.random.normal(k[6], (C, HS), jnp.float32) * s, 'Ws3': jax.random.normal(k[7], (HS, C), jnp.float32) * s}
    _L0_ffn_all = _L0_ffn_setup()
    _L0_ffn_in = {k: v for k, v in _L0_ffn_all.items() if k in ('Wg', 'W1', 'W2', 'W3', 'Ws1', 'Ws2', 'Ws3')}
    del _L0_ffn_all
    return {'x': x, 'ctx_1024': ctx_1024, 'mask_BxSxS2_bf0': mask_BxSxS2_bf0, 'L0_attn_ln_g': _L0_attn_in['ln_g'], 'L0_attn_ln_b': _L0_attn_in['ln_b'], 'L0_attn_w_qkvb': _L0_attn_in['w_qkvb'], 'L0_attn_b_qkvb': _L0_attn_in['b_qkvb'], 'L0_attn_w_out': _L0_attn_in['w_out'], 'L0_attn_b_out': _L0_attn_in['b_out'], 'L0_xattn_Wq': _L0_xattn_in['Wq'], 'L0_xattn_Wk': _L0_xattn_in['Wk'], 'L0_xattn_Wv': _L0_xattn_in['Wv'], 'L0_xattn_Wr': _L0_xattn_in['Wr'], 'L0_xattn_ub_w': _L0_xattn_in['ub_w'], 'L0_xattn_vb_w': _L0_xattn_in['vb_w'], 'L0_xattn_head_w': _L0_xattn_in['head_w'], 'L0_xattn_Wo': _L0_xattn_in['Wo'], 'L0_xattn_ln_g': _L0_xattn_in['ln_g'], 'L0_xattn_ln_b': _L0_xattn_in['ln_b'], 'L0_ffn_Wg': _L0_ffn_in['Wg'], 'L0_ffn_W1': _L0_ffn_in['W1'], 'L0_ffn_W2': _L0_ffn_in['W2'], 'L0_ffn_W3': _L0_ffn_in['W3'], 'L0_ffn_Ws1': _L0_ffn_in['Ws1'], 'L0_ffn_Ws2': _L0_ffn_in['Ws2'], 'L0_ffn_Ws3': _L0_ffn_in['Ws3']}

def reference(x, ctx_1024, mask_BxSxS2_bf0, L0_attn_ln_g, L0_attn_ln_b, L0_attn_w_qkvb, L0_attn_b_qkvb, L0_attn_w_out, L0_attn_b_out, L0_xattn_Wq, L0_xattn_Wk, L0_xattn_Wv, L0_xattn_Wr, L0_xattn_ub_w, L0_xattn_vb_w, L0_xattn_head_w, L0_xattn_Wo, L0_xattn_ln_g, L0_xattn_ln_b, L0_ffn_Wg, L0_ffn_W1, L0_ffn_W2, L0_ffn_W3, L0_ffn_Ws1, L0_ffn_Ws2, L0_ffn_Ws3):
    import jax
    import jax.numpy as jnp

    def _L0_attn_ref(x, ln_g, ln_b, w_qkvb, b_qkvb, w_out, b_out):
        import jax, jax.numpy as jnp
        import numpy as np
        from jax import lax
        B, T, HID, NH = (4, 256, 128, 16)
        D = HID // NH
        LN_EPS = 1e-05
        NORM_EPS = 1e-06
        b, t = x.shape[:2]
        mu = jnp.mean(x, axis=-1, keepdims=True)
        var = jnp.mean((x - mu) ** 2, axis=-1, keepdims=True)
        normed = (x - mu) * lax.rsqrt(var + LN_EPS) * ln_g + ln_b
        proj = normed @ w_qkvb + b_qkvb
        q, k, v, beta_pre = jnp.split(proj, 4, axis=-1)
        beta = jax.nn.sigmoid(beta_pre)

        def heads(a):
            return a.reshape(b, t, NH, D).transpose(1, 0, 2, 3)
        q, k, v, beta = (heads(q), heads(k), heads(v), heads(beta))
        k = k / jnp.maximum(jnp.linalg.norm(k, axis=-1, keepdims=True), NORM_EPS)
        S0 = jnp.zeros((b, NH, D, D), x.dtype)

        def step(S, inp):
            q_t, k_t, v_t, beta_t = inp
            retrieval = jnp.einsum('bhij,bhj->bhi', S, k_t)
            S = S + jnp.einsum('bhi,bhj->bhij', beta_t * (v_t - retrieval), k_t)
            o_t = jnp.einsum('bhij,bhj->bhi', S, q_t)
            return (S, o_t)
        _, out_t = lax.scan(step, S0, (q, k, v, beta))
        scan_out = out_t.transpose(1, 0, 2, 3).reshape(b, t, NH * D)
        return x + scan_out @ w_out + b_out

    def _L0_xattn_ref(q, k, v, attn_mask, Wq, Wk, Wv, Wr, ub_w, vb_w, head_w, Wo, ln_g, ln_b):
        import jax, jax.numpy as jnp
        import numpy as np
        D_MODEL = 128
        N_HEADS = 16
        D_K = 64
        D_V = 64
        INIT_RANGE = 0.1
        INF = 1000000000.0
        B, L = (8, 64)

        def _pos_emb(pos):
            d = D_MODEL
            freq = 1.0 / 10000.0 ** (jnp.arange(0, d, 2, dtype=jnp.float32) / d)
            ang = pos[:, None] * freq[None, :]
            scale = INIT_RANGE * d
            emb = jnp.stack([jnp.sin(ang) * scale, jnp.cos(ang) * scale], axis=-1)
            return emb.reshape(pos.shape[0], d)
        Bq, Lq, _ = q.shape
        Lk = k.shape[1]
        residual = q
        rpos = jnp.arange(Lq - 1, -Lk, -1).astype(jnp.float32)
        head_r = (_pos_emb(rpos) @ Wr).reshape(-1, D_V, N_HEADS)
        hq = (q @ Wq).reshape(Bq, Lq, D_K, N_HEADS)
        hk = (k @ Wk).reshape(Bq, Lk, D_K, N_HEADS)
        hv = (v @ Wv).reshape(Bq, Lk, D_V, N_HEADS)
        attn = jnp.einsum('bidn,bjdn->bijn', hq, hk)
        idx = Lq - 1 - jnp.arange(Lq)[:, None] + jnp.arange(Lk)[None, :]
        b_full = jnp.einsum('bidn,jdn->bijn', hq, head_r)
        attn = attn + jnp.take_along_axis(b_full, idx[None, :, :, None], axis=2)
        attn = attn + jnp.einsum('bjdn,d->bjn', hk, ub_w)[:, None, :, :]
        d_full = jnp.einsum('jdn,d->jn', head_r, vb_w)
        attn = attn + d_full[idx][None]
        attn = attn / jnp.sqrt(jnp.asarray(D_MODEL, attn.dtype))
        attn = jnp.where(attn_mask[..., None], -INF, attn)
        attn = jax.nn.softmax(attn, axis=2)
        out = jnp.einsum('bijn,bjdn->bidn', attn, hv)
        hw = jax.nn.sigmoid(q @ head_w)
        out = out * hw[:, :, None, :]
        out = out.reshape(Bq, Lq, D_V * N_HEADS) @ Wo + residual
        mean = out.mean(-1, keepdims=True)
        var = out.var(-1, keepdims=True)
        return (out - mean) / jnp.sqrt(var + 1e-05) * ln_g + ln_b

    def _L0_ffn_ref(x, Wg, W1, W2, W3, Ws1, Ws2, Ws3):
        import jax, jax.numpy as jnp
        import numpy as np
        B, T, C = (4, 256, 128)
        E = 8
        K = 2
        H = 176
        HS = 176 * 2
        b, t, c = x.shape
        xf = x.reshape(-1, c)
        n = xf.shape[0]
        router = xf @ Wg
        top_logits, idx = jax.lax.top_k(router, K)
        probs = jax.nn.softmax(top_logits.astype(jnp.float32), axis=-1).astype(x.dtype)
        w = jnp.zeros((n, E), x.dtype).at[jnp.arange(n)[:, None], idx].add(probs)
        h = jax.nn.silu(jnp.einsum('tc,ech->eth', xf, W1)) * jnp.einsum('tc,ech->eth', xf, W2)
        y = jnp.einsum('eth,ehc,te->tc', h, W3, w)
        y = y.reshape(b, t, c)
        hs = jax.nn.silu(xf @ Ws1) * (xf @ Ws2)
        y = y + (hs @ Ws3).reshape(b, t, c)
        return y
    x = x + _L0_attn_ref(_layernorm(x, axis=-1), L0_attn_ln_g, L0_attn_ln_b, L0_attn_w_qkvb, L0_attn_b_qkvb, L0_attn_w_out, L0_attn_b_out)
    x = x + _L0_xattn_ref(_layernorm(x, axis=-1), ctx_1024, ctx_1024, mask_BxSxS2_bf0, L0_xattn_Wq, L0_xattn_Wk, L0_xattn_Wv, L0_xattn_Wr, L0_xattn_ub_w, L0_xattn_vb_w, L0_xattn_head_w, L0_xattn_Wo, L0_xattn_ln_g, L0_xattn_ln_b)
    x = x + _L0_ffn_ref(_layernorm(x, axis=-1), L0_ffn_Wg, L0_ffn_W1, L0_ffn_W2, L0_ffn_W3, L0_ffn_Ws1, L0_ffn_Ws2, L0_ffn_Ws3)
    return x

_drawn_inputs = setup_inputs


def setup_inputs(seed=0):
    import zlib

    import numpy as np

    out = dict(_drawn_inputs(seed))
    spreads = {'L0_attn_ln_g': (1.0, 0.6),
     'L0_attn_ln_b': (0.0, 0.8),
     'L0_attn_b_qkvb': (0.0, 0.8),
     'L0_attn_b_out': (0.0, 0.353),
     'L0_xattn_ln_g': (1.0, 0.2),
     'L0_xattn_ln_b': (0.0, 0.27)}
    factors = {'L0_attn_w_qkvb': 4.453,
     'L0_attn_w_out': 4.4,
     'L0_xattn_Wk': 3.673,
     'L0_xattn_ub_w': 8.0,
     'L0_xattn_vb_w': 8.0,
     'L0_ffn_Wg': 8.0,
     'L0_ffn_W1': 8.0,
     'L0_ffn_W2': 8.0,
     'L0_ffn_W3': 8.0,
     'L0_ffn_Ws1': 8.0,
     'L0_ffn_Ws2': 8.0,
     'L0_ffn_Ws3': 8.0}
    for name, (base, spread) in spreads.items():
        noise = np.random.default_rng([zlib.crc32(name.encode()), seed]).standard_normal(out[name].shape)
        drawn = base * np.exp(spread * noise) if base else spread * noise
        out[name] = jnp.asarray(drawn.astype(out[name].dtype))
    for name, factor in factors.items():
        out[name] = (out[name] * factor).astype(out[name].dtype)
    return out
```

```python
import concourse.bass as bass
from concourse import mybir
from contextlib import ExitStack

B, T, C = 8, 128, 128
NH, DH = 16, 8
CH = 32
NC = T // CH
J = 120
XH, DK = 16, 64
PAIRS = XH // 2
GB = 4
NG = B // GB
GT = GB * T
NREL = T + J - 1
EXP, HID = 8, 176
REST = HID - 128
SHID = 352
HCH = EXP + EXP // 2 + 3
BANK = 512
LN_EPS = 1e-5
NORM_EPS = 1e-6
SCALE = float(C) ** -0.5
NEG = -1.0e9


def layer(nc, x, ctxT, maskT, w_qkvb, w_out, cols, rows, consts, Wq, Wk, Wv, WrT, Wo, head_w, rel_tab,
          Wg, W1, W2, W3, out):
    fp32 = mybir.dt.float32
    u8 = mybir.dt.uint8
    ALU = mybir.AluOpType
    ACT = mybir.ActivationFunctionType
    AX = mybir.AxisListType.X

    ctx = ExitStack()
    with ctx:
        def sb(name, shape, dt=fp32):
            return ctx.enter_context(nc.sbuf_tensor(name, shape, dt))

        def sem(name):
            return ctx.enter_context(nc.semaphore(name))

        hk = sb("hk", [128, PAIRS, B, J])
        hv = sb("hv", [J, B, XH * DK])
        xs = sb("xs", [128, B, C])
        qn = sb("qn", [128, B, C])
        qT = sb("qT", [128, B * T])
        Wq_s = sb("Wq_s", [128, XH * DK])
        WrT_s = sb("WrT_s", [128, PAIRS, C])
        Wo_s = sb("Wo_s", [128, PAIRS, C])
        rel_s = sb("rel_s", [128, NREL])
        ident = sb("ident", [128, 128])
        same_head = sb("same_head", [128, 128])
        hw_s = sb("hw_s", [128, XH])
        Wg_s = sb("Wg_s", [128, EXP])
        rows_s = sb("rows_s", [128, 3, C])
        cols_s = sb("cols_s", [128, 8])
        maskadd = sb("maskadd", [J, B, T])
        mask_s = sb("mask_s", [J, B, T], u8)
        small = sb("small", [128, 16])
        relb = sb("relb", [128, XH])
        st = sb("st", [128, B, 6])
        mv = sb("mv", [128, B, 2])
        rs = sb("rs", [128, B])
        var = sb("var", [128, B])
        neg_half = sb("neg_half", [128, B])
        nmax = sb("nmax", [128, XH * B])
        rsum = sb("rsum", [128, XH * B])
        gate = sb("gate", [128, GB, XH])
        rden = sb("rden", [128, XH])
        rt = sb("rt", [128, 12, GB, EXP])
        pw = sb("pw", [128, B, EXP])

        REGION = 27000
        region = sb("region", [128, REGION])
        at = [0]

        def cut(*shape, p=128):
            n = 1
            for s in shape:
                n *= s
            a = region[0:p, at[0]:at[0] + n]
            at[0] += n
            assert at[0] <= REGION, at[0]
            names = "abcd"[:len(shape)]
            if len(shape) == 1:
                return a
            return a.rearrange(f"p ({' '.join(names)}) -> p {' '.join(names)}",
                               **dict(zip(names, shape)))

        kx = cut(2, CH, B, DH + 1)
        bk = cut(2, CH, B, DH)
        qx = cut(2, CH, B, DH)
        hist = cut(CH, B, DH + 1)
        xn = cut(B, C)
        z = cut(B, C)
        nT = cut(B * T)
        kT = cut(B * T)
        vT = cut(B * T)
        nbeta = cut(B * T)
        sq = z.rearrange("p b t -> p (b t)")
        attT = sq
        sel = cut(DH, 128)
        wqkvb_s = cut(4 * C)
        wout_s = cut(C)
        Wk_s = cut(XH * DK)
        Wv_s = cut(XH * DK)
        ctxT_s = cut(B, J)
        prod = cut(B, DH + 1)
        delta = cut(B)
        outer = cut(B, DH)
        at[0] = 0
        wrel = cut(T, GB * XH)
        relT = cut(GB * XH, T, p=J)
        hqu = cut(PAIRS, GT)
        pbuf = cut(4, 4, J)
        pT = cut(4, 4, T, p=J)
        osc = cut(XH * DK)
        oT = cut(PAIRS, T)
        at[0] = 0
        W1_s = cut(HCH, 128)
        W2_s = cut(HCH, 128)
        W3_s = cut(HCH, C)
        hid = cut(HCH, GT)
        gact = cut(4, GT)
        y3 = cut(B, C)

        ps = ctx.enter_context(nc.psum_tensor("ps", [128, 8, BANK], fp32))

        ld = {n: sem("ld_" + n) for n in
              ["x", "cols", "rows", "consts", "sel", "wqkvb", "wout", "ctx", "Wk", "Wv", "Wq", "Wr", "Wo",
               "tail", "mask", "moe"]}
        z_ready = sem("z_ready")
        zT_ps = sem("zT_ps")
        nT_ready = sem("nT_ready")
        proj_ps = sem("proj_ps")
        proj_ev = sem("proj_ev")
        norm_ps = sem("norm_ps")
        kn_ready = sem("kn_ready")
        small_ready = sem("small_ready")
        var_ready = sem("var_ready")
        rs_ready = sem("rs_ready")
        nrm_ready = sem("nrm_ready")
        spread_ps = sem("spread_ps")
        spread_ev = sem("spread_ev")
        kx_ready = sem("kx_ready")
        scan_step = sem("scan_step")
        scan_done = sem("scan_done")
        qs_ready = sem("qs_ready")
        att_ps = sem("att_ps")
        att_ev = sem("att_ev")
        ctxp_ps = sem("ctxp_ps")
        ctxp_ev = sem("ctxp_ev")
        xn_ready = sem("xn_ready")
        base_ready = sem("base_ready")
        relb_ps = sem("relb_ps")
        relb_ready = sem("relb_ready")
        x2_ps = sem("x2_ps")
        qn_ready = sem("qn_ready")
        qnT_ps = sem("qnT_ps")
        qT_ready = sem("qT_ready")
        hq_ps = sem("hq_ps")
        hq_ev = sem("hq_ev")
        w_ps = sem("w_ps")
        w_ev = sem("w_ev")
        rel_ps = sem("rel_ps")
        rel_ev = sem("rel_ev")
        s_ps = sem("s_ps")
        max_ready = sem("max_ready")
        p_ready = sem("p_ready")
        pT_ps = sem("pT_ps")
        pT_ready = sem("pT_ready")
        o_ps = sem("o_ps")
        gate_ps = sem("gate_ps")
        gate_t = sem("gate_t")
        osc_ready = sem("osc_ready")
        oT_ps = sem("oT_ps")
        oT_ready = sem("oT_ready")
        y_ps = sem("y_ps")
        y_ready = sem("y_ready")
        z3_ready = sem("z3_ready")
        z3T_ps = sem("z3T_ps")
        z3T_ready = sem("z3T_ready")
        route_ps = sem("route_ps")
        route_sub = sem("route_sub")
        route_exp = sem("route_exp")
        up_ps = sem("up_ps")
        act_ready = sem("act_ready")
        hid_ready = sem("hid_ready")
        down_ps = sem("down_ps")
        down_used = sem("down_used")
        stored = sem("stored")
        vec = sem("vec")
        pool_own = sem("pool_own")

        CTX_UNITS = [("k", g, p) for g in range(NG) for p in range(PAIRS)] + \
                    [("v", b, h) for b in range(B) for h in range(2)]
        CTX_SPLIT = 16

        def head(q4, h):
            return 8 * (q4 // 2) + 2 * h + q4 % 2

        def expert(m, e):
            return 2 * e + m - 1

        block = ctx.enter_context(nc.Block())

        @block.sync
        def _(sp):
            sp.dma_start(xs[:, :, :], x.rearrange("b t c -> t b c")).then_inc(ld["x"], 16)
            sp.dma_start(cols_s[:, :], cols).then_inc(ld["cols"], 16)
            sp.dma_start(ident[:, :], consts[:, 0:128]).then_inc(ld["consts"], 16)
            sp.dma_start(wqkvb_s, w_qkvb).then_inc(ld["wqkvb"], 16)
            sp.dma_start(same_head[:, :], consts[:, 128:256]).then_inc(ld["consts"], 16)
            sp.dma_start(sel.rearrange("p a b -> p (a b)"), consts[:, 256:256 + DH * 128]).then_inc(ld["sel"], 16)
            sp.dma_start(ctxT_s, ctxT).then_inc(ld["ctx"], 16)
            sp.dma_start(Wk_s, Wk).then_inc(ld["Wk"], 16)
            sp.dma_start(Wv_s, Wv).then_inc(ld["Wv"], 16)
            sp.dma_start(wout_s, w_out).then_inc(ld["wout"], 16)
            sp.dma_start(rows_s[:, :, :].rearrange("p a c -> p (a c)"),
                         rows.rearrange("a c -> (a c)").partition_broadcast(128)).then_inc(ld["rows"], 16)
            sp.dma_start(WrT_s[:, :, :], WrT).then_inc(ld["Wr"], 16)
            sp.dma_start(Wq_s[:, :], Wq).then_inc(ld["Wq"], 16)
            sp.dma_start(mask_s[:, :, :], maskT).then_inc(ld["mask"], 16)
            sp.dma_start(rel_s[:, :], rel_tab).then_inc(ld["tail"], 16)
            sp.dma_start(hw_s[:, :], head_w).then_inc(ld["tail"], 16)
            sp.dma_start(Wg_s[:, :], Wg).then_inc(ld["tail"], 16)
            sp.dma_start(Wo_s[:, :, :], Wo).then_inc(ld["Wo"], 16)
            sp.wait_ge(rel_ps, NG * T // 8)
            sp.dma_start(W1_s, W1).then_inc(ld["moe"], 16)
            sp.dma_start(W2_s, W2).then_inc(ld["moe"], 16)
            sp.dma_start(W3_s, W3).then_inc(ld["moe"], 16)
            for b in range(B):
                sp.wait_ge(down_used, 3 * (b + 1))
                sp.dma_start(out[b, :, :], y3[:, b, :]).then_inc(stored, 16)
            sp.wait_ge(stored, 16 * B)

        @block.gpsimd
        def _(pool):
            nc.gpsimd.memset(neg_half[:, :], -0.5).then_inc(pool_own, 1)
            pool.wait_ge(pool_own, 1)

            def inverse_roots(i, b0=0, b1=B):
                pool.wait_ge(var_ready, i + 1)
                nc.gpsimd.tensor_tensor(rs[:, b0:b1], var[:, b0:b1], neg_half[:, b0:b1], ALU.pow).then_inc(rs_ready, 1)

            inverse_roots(0)
            inverse_roots(1)
            pool.wait_ge(ld["x"], 16)
            pool.wait_ge(ld["rows"], 16)
            pool.wait_ge(xn_ready, B)
            nc.gpsimd.tensor_tensor(xs[:, :, :], xs[:, :, :], xn, ALU.add).then_inc(pool_own, 1)
            pool.wait_ge(pool_own, 2)
            nc.gpsimd.tensor_tensor(xs[:, :, :], xs[:, :, :],
                                    rows_s[:, 0:1, :].to_broadcast([128, B, C]), ALU.add).then_inc(base_ready, 1)
            inverse_roots(2)
            for g in range(NG):
                inverse_roots(3 + 2 * g, g * GB, (g + 1) * GB)
                inverse_roots(4 + 2 * g, g * GB, (g + 1) * GB)

        @block.scalar
        def _(act):
            act.wait_ge(ld["cols"], 16)
            for h in range(2):
                act.wait_ge(zT_ps, h + 1)
                nc.scalar.activation(nT[:, h * GT:(h + 1) * GT], ps[:, h, :], ACT.Identity,
                                     scale=cols_s[:, 0:1], bias=cols_s[:, 1:2]).then_inc(nT_ready, 1)
            for h in range(2):
                act.wait_ge(proj_ps, h + 1)
                nc.scalar.activation(sq[:, h * GT:(h + 1) * GT], ps[:, 2 + h, :], ACT.Square,
                                     bias=cols_s[:, 3:4])
                nc.scalar.activation(kT[:, h * GT:(h + 1) * GT], ps[:, 2 + h, :], ACT.Identity,
                                     bias=cols_s[:, 3:4]).then_inc(proj_ev, 1)
            for h in range(2):
                act.wait_ge(proj_ps, 3 + h)
                nc.scalar.activation(vT[:, h * GT:(h + 1) * GT], ps[:, 6 + h, :], ACT.Identity,
                                     bias=cols_s[:, 4:5]).then_inc(proj_ev, 1)
            for h in range(2):
                act.wait_ge(norm_ps, h + 1)
                nc.scalar.activation(sq[:, h * GT:(h + 1) * GT], ps[:, 2 + h, :], ACT.Sqrt).then_inc(nrm_ready, 1)
            for h in range(2):
                act.wait_ge(proj_ps, 5 + h)
                nc.scalar.activation(qT[:, h * GT:(h + 1) * GT], ps[:, h, :], ACT.Identity,
                                     bias=cols_s[:, 2:3]).then_inc(proj_ev, 1)
            act.wait_ge(small_ready, 1)
            for h in range(2):
                act.wait_ge(proj_ps, 7 + h)
                nc.scalar.activation(nbeta[:, h * GT:(h + 1) * GT], ps[:, 4 + h, :], ACT.Tanh,
                                     bias=small[:, 0:1], scale=0.5).then_inc(proj_ev, 1)

            def spread_out(c):
                if c >= 2:
                    act.wait_ge(scan_done, c - 1)
                for u in range(2):
                    act.wait_ge(spread_ps, 4 * c + u + 1)
                    for s in range(2):
                        ins = nc.scalar.activation(
                            kx[:, c % 2, :, :, 4 * u + 2 * s:4 * u + 2 * s + 2].rearrange("p t b j -> p j b t"),
                            ps[:, 2 * u + s, :].rearrange("p (j b t) -> p j b t", j=2, b=B),
                            ACT.Copy, scale=-1.0)
                    ins.then_inc(spread_ev, 1)
                if c == 0:
                    act.wait_ge(proj_ev, 4)
                nc.scalar.activation(kx[:, c % 2, :, :, DH].rearrange("p t b -> p b t"),
                                     vT.rearrange("p (b t) -> p b t", b=B)[:, :, c * CH:(c + 1) * CH],
                                     ACT.Copy).then_inc(kx_ready, 1)
                if c >= 2:
                    act.wait_ge(att_ps, c - 1)
                for u in range(2):
                    act.wait_ge(spread_ps, 4 * c + u + 3)
                    for s in range(2):
                        ins = nc.scalar.activation(
                            qx[:, c % 2, :, :, 4 * u + 2 * s:4 * u + 2 * s + 2].rearrange("p t b j -> p j b t"),
                            ps[:, 2 * u + s, :].rearrange("p (j b t) -> p j b t", j=2, b=B), ACT.Copy)
                    ins.then_inc(spread_ev, 1)

            def ctx_out(i):
                kind, a, h = CTX_UNITS[i]
                act.wait_ge(ctxp_ps, i + 1)
                if kind == "k":
                    nc.scalar.activation(hk[:, h, a * GB:(a + 1) * GB, :],
                                         ps[:, 4 + i % 3, 0:GB * J].rearrange("p (b j) -> p b j", b=GB),
                                         ACT.Copy).then_inc(ctxp_ev, 1)
                else:
                    nc.scalar.activation(hv[:, a, h * BANK:(h + 1) * BANK], ps[0:J, 4 + i % 3, :],
                                         ACT.Copy).then_inc(ctxp_ev, 1)

            def att_out(c):
                act.wait_ge(att_ps, c + 1)
                nc.scalar.activation(attT.rearrange("p (b t) -> p b t", b=B)[:, :, c * CH:(c + 1) * CH],
                                     ps[:, 7, (c % 2) * 256:(c % 2) * 256 + 256]
                                     .rearrange("p (b t) -> p b t", b=B), ACT.Copy).then_inc(att_ev, 1)

            spread_out(0)
            act.wait_ge(relb_ps, 1)
            for r in range(2):
                nc.scalar.activation(relb[:, r:XH:2], ps[:, 6 + r, r:XH:2], ACT.Copy).then_inc(relb_ready, 1)
            spread_out(1)
            for i in range(CTX_SPLIT):
                ctx_out(i)
            att_out(0)
            spread_out(2)
            for i in range(CTX_SPLIT, len(CTX_UNITS)):
                ctx_out(i)
            att_out(1)
            spread_out(3)
            att_out(2)
            att_out(3)

            for h in range(2):
                act.wait_ge(qnT_ps, h + 1)
                nc.scalar.activation(qT[:, h * GT:(h + 1) * GT], ps[:, 2 + h, :], ACT.Copy).then_inc(qT_ready, 1)
            for g in range(NG):
                for p in range(PAIRS):
                    act.wait_ge(hq_ps, g * PAIRS + p + 1)
                    nc.scalar.activation(hqu[:, p, :], ps[:, p % 4, :], ACT.Identity,
                                         scale=SCALE, bias=small[:, 1:2]).then_inc(hq_ev, 1)
                act.wait_ge(relb_ready, 2)
                for n in range(XH):
                    act.wait_ge(w_ps, g * XH + n + 1)
                    nc.scalar.activation(
                        wrel.rearrange("p i (b n) -> p b i n", n=XH)[:, :, :, n],
                        ps[:, n % 4, :].rearrange("p (b i) -> p b i", b=GB),
                        ACT.Identity, bias=relb[:, n:n + 1]).then_inc(w_ev, 1)
                act.wait_ge(gate_ps, g + 1)
                nc.scalar.activation(gate[:, :, :],
                                     ps[:, 7, 128:128 + GB * XH].rearrange("p (b n) -> p b n", b=GB),
                                     ACT.Tanh, scale=0.5).then_inc(gate_t, 1)
                first, last = g * GB * 4, (g + 1) * GB * 4
                for k in range(first, last + 2):
                    if k < last:
                        b, q4 = k // 4, k % 4
                        act.wait_ge(max_ready, k + 1)
                        if k >= 4:
                            act.wait_ge(pT_ps, k - 3)
                        for h in range(4):
                            n = b * XH + head(q4, h)
                            ins = nc.scalar.activation(pbuf[:, k % 4, h, :], ps[:, k % 2, h * J:(h + 1) * J],
                                                       ACT.Exp, bias=nmax[:, 4 * k + h:4 * k + h + 1],
                                                       accum_out=rsum[:, n:n + 1])
                        ins.then_inc(p_ready, 1)
                    if k % 4 == 1 and k > first + 4:
                        for h in range(2):
                            act.wait_ge(oT_ps, 2 * (k // 4 - 1) + h + 1)
                            nc.scalar.activation(oT[:, 4 * h:4 * h + 4, :],
                                                 ps[:, 6, :].rearrange("p (a i) -> p a i", a=4),
                                                 ACT.Copy).then_inc(oT_ready, 1)

            for g in range(NG):
                act.wait_ge(z3T_ps, g + 1)
                nc.scalar.activation(qT[:, g * GT:(g + 1) * GT], ps[:, 4 + g, :], ACT.Copy).then_inc(z3T_ready, 1)
            for g in range(NG):
                act.wait_ge(route_sub, g + 1)
                nc.scalar.activation(rt[:, 2, :, :], rt[:, 1, :, :], ACT.Exp).then_inc(route_exp, 1)
                for i in range(HCH):
                    u = g * HCH + i
                    act.wait_ge(up_ps, u + 1)
                    if u >= 4:
                        act.wait_ge(hid_ready, u - 3)
                    nc.scalar.activation(gact[:, u % 4, :], ps[:, (u % 2) * 2, :], ACT.Silu).then_inc(act_ready, 1)

        @block.vector
        def _(dve):
            count = [0]

            norms = [0]

            def own(ins):
                ins.then_inc(vec, 1)
                count[0] += 1

            def settle():
                dve.wait_ge(vec, count[0])

            def layernorm_stats(src, b0, b1):
                for b in range(b0, b1):
                    own(nc.vector.bn_stats(st[:, b, :], src[:, b, :]))
                settle()
                for b in range(b0, b1):
                    own(nc.vector.bn_aggr(mv[:, b, :], st[:, b, :]))
                settle()
                nc.vector.tensor_scalar(var[:, b0:b1], mv[:, b0:b1, 1], LN_EPS, None, ALU.add).then_inc(var_ready, 1)
                norms[0] += 1
                dve.wait_ge(rs_ready, norms[0])

            def layernorm(dst, src, b0, b1, ready=None):
                layernorm_stats(src, b0, b1)
                for b in range(b0, b1):
                    ins = nc.vector.tensor_scalar(dst[:, b, :], src[:, b, :], mv[:, b, 0:1], rs[:, b:b + 1],
                                                  ALU.subtract, ALU.mult)
                    if ready is not None:
                        ins.then_inc(ready, 1)
                    else:
                        own(ins)

            own(nc.vector.memset(hist[:, :, :, :], 0.0))
            settle()
            own(nc.vector.memset(hist[:, :, :, DH], 1.0))
            dve.wait_ge(ld["cols"], 16)
            nc.vector.tensor_scalar(small[:, 0:1], cols_s[:, 5:6], 0.5, None, ALU.mult)
            own(nc.vector.tensor_scalar(small[:, 1:2], cols_s[:, 6:7], SCALE, None, ALU.mult))
            own(nc.vector.tensor_tensor(small[:, 2:3], cols_s[:, 7:8], cols_s[:, 6:7], ALU.subtract))
            settle()
            nc.vector.tensor_scalar(small[:, 3:4], small[:, 2:3], SCALE, None, ALU.mult).then_inc(small_ready, 1)

            dve.wait_ge(ld["x"], 16)
            layernorm(xn, xs, 0, B, xn_ready)
            dve.wait_ge(xn_ready, B)
            layernorm(z, xn, 0, B, z_ready)

            for h in range(2):
                dve.wait_ge(nrm_ready, h + 1)
                own(nc.vector.tensor_scalar(sq[:, h * GT:(h + 1) * GT], sq[:, h * GT:(h + 1) * GT], NORM_EPS,
                                            None, ALU.max))
                settle()
                own(nc.vector.reciprocal(sq[:, h * GT:(h + 1) * GT], sq[:, h * GT:(h + 1) * GT]))
                settle()
                dve.wait_ge(proj_ev, h + 1)
                nc.vector.tensor_tensor(kT[:, h * GT:(h + 1) * GT], kT[:, h * GT:(h + 1) * GT],
                                        sq[:, h * GT:(h + 1) * GT], ALU.mult).then_inc(kn_ready, 1)
            dve.wait_ge(proj_ev, 8)
            own(nc.vector.tensor_scalar(nbeta, nbeta, -0.5, -0.5, ALU.mult, ALU.add))
            settle()
            dve.wait_ge(ld["mask"], 16)
            own(nc.vector.tensor_scalar(maskadd[:, :, :], mask_s[:, :, :], NEG, None, ALU.mult))

            nb = nbeta.rearrange("p (b t) -> p t b", b=B)
            for c in range(NC):
                s = c % 2
                dve.wait_ge(kx_ready, c + 1)
                own(nc.vector.tensor_tensor(
                    bk[:, s, :, :, :], kx[:, s, :, :, 0:DH],
                    nb[:, c * CH:(c + 1) * CH, :].unsqueeze(3).to_broadcast([128, CH, B, DH]), ALU.mult))
                settle()
                for t in range(CH):
                    step = 4 * (c * CH + t)
                    before, after = (t - 1) % CH, t
                    if step:
                        dve.wait_ge(scan_step, step)
                    nc.vector.tensor_tensor(prod, hist[:, before, :, :], kx[:, s, t, :, :],
                                            ALU.mult).then_inc(scan_step, 1)
                    dve.wait_ge(scan_step, step + 1)
                    nc.vector.tensor_reduce(delta, prod, AX, ALU.add).then_inc(scan_step, 1)
                    dve.wait_ge(scan_step, step + 2)
                    nc.vector.tensor_tensor(outer, bk[:, s, t, :, :],
                                            delta.unsqueeze(2).to_broadcast([128, B, DH]),
                                            ALU.mult).then_inc(scan_step, 1)
                    dve.wait_ge(scan_step, step + 3)
                    nc.vector.tensor_tensor(hist[:, after, :, 0:DH], hist[:, before, :, 0:DH], outer,
                                            ALU.add).then_inc(scan_step, 1)
                dve.wait_ge(scan_step, 4 * (c + 1) * CH)
                dve.wait_ge(spread_ev, 4 * c + 4)
                nc.vector.tensor_tensor(qx[:, s, :, :, :], hist[:, :, :, 0:DH], qx[:, s, :, :, :],
                                        ALU.mult).then_inc(scan_done, 1)

            dve.wait_ge(base_ready, 1)
            for h in range(2):
                dve.wait_ge(x2_ps, h + 1)
                own(nc.vector.tensor_tensor(xs[:, h * GB:(h + 1) * GB, :], xs[:, h * GB:(h + 1) * GB, :],
                                            ps[:, h, :].rearrange("p (b c) -> p b c", b=GB), ALU.add))
            settle()

            layernorm(qn, xs, 0, B, qn_ready)

            def tail(b):
                bl = b % GB
                own(nc.vector.reciprocal(rden[:, :], rsum[:, b * XH:(b + 1) * XH]))
                settle()
                own(nc.vector.tensor_tensor(gate[:, bl, :], gate[:, bl, :], rden[:, :], ALU.mult))
                settle()
                dve.wait_ge(o_ps, 4 * (b + 1))
                if b >= 1:
                    dve.wait_ge(oT_ps, 2 * b)
                for h in range(2):
                    nc.vector.tensor_tensor(
                        osc[:, h * BANK:(h + 1) * BANK].rearrange("p (n d) -> p n d", d=DK),
                        ps[:, 4 + h, :].rearrange("p (n d) -> p n d", d=DK),
                        gate[:, bl, 8 * h:8 * h + 8].unsqueeze(2).to_broadcast([128, 8, DK]),
                        ALU.mult).then_inc(osc_ready, 1)

            def finish(b):
                dve.wait_ge(y_ps, b + 1)
                nc.vector.tensor_tensor(qn[:, b, :], qn[:, b, :], ps[:, 7, 0:C], ALU.add).then_inc(y_ready, 1)

            for g in range(NG):
                for i8 in range(T // 8):
                    u = g * (T // 8) + i8
                    dve.wait_ge(rel_ps, u + 1)
                    if i8 == 0 and g:
                        dve.wait_ge(s_ps, g * GB * 4)
                    nc.vector.tensor_tensor(
                        relT[:, :, 8 * i8:8 * i8 + 8].rearrange("p (b n) i -> p i b n", b=GB),
                        ps[0:J, i8 % 4, :].rearrange("p (i b n) -> p i b n", i=8, b=GB),
                        maskadd[:, g * GB:(g + 1) * GB, 8 * i8:8 * i8 + 8]
                        .rearrange("p b i -> p i b").unsqueeze(3).to_broadcast([J, 8, GB, XH]),
                        ALU.add).then_inc(rel_ev, 1)
                first, last = g * GB * 4, (g + 1) * GB * 4
                dve.wait_ge(gate_t, g + 1)
                own(nc.vector.tensor_scalar(gate[:, :, :], gate[:, :, :], 0.5, 0.5, ALU.mult, ALU.add))
                settle()
                for k in range(first, last + 3):
                    if k < last:
                        dve.wait_ge(s_ps, k + 1)
                        nc.vector.tensor_reduce(nmax[:, 4 * k:4 * k + 4],
                                                ps[:, k % 2, 0:4 * J].rearrange("p (h j) -> p h j", h=4),
                                                AX, ALU.max, negate=True).then_inc(max_ready, 1)
                    if first < k <= last:
                        dve.wait_ge(pT_ps, k)
                        if k - 1 >= 4:
                            dve.wait_ge(o_ps, k - 4)
                        nc.vector.tensor_copy(pT[:, (k - 1) % 4, :, :],
                                              ps[0:J, 2 + (k - 1) % 2, :].rearrange("p (h i) -> p h i", h=4)
                                              ).then_inc(pT_ready, 1)
                    if k % 4 == 1 and k > first + 4:
                        tail(k // 4 - 1)
                    if k % 4 == 2 and k > first + 4:
                        finish(k // 4 - 1)
                dve.wait_ge(y_ready, (g + 1) * GB)
                b0, b1 = g * GB, (g + 1) * GB
                layernorm(qn, qn, b0, b1)
                settle()
                own(nc.vector.tensor_tensor(qn[:, b0:b1, :], qn[:, b0:b1, :],
                                            rows_s[:, 1:2, :].to_broadcast([128, GB, C]), ALU.mult))
                settle()
                own(nc.vector.tensor_tensor(qn[:, b0:b1, :], qn[:, b0:b1, :],
                                            rows_s[:, 2:3, :].to_broadcast([128, GB, C]), ALU.add))
                settle()
                own(nc.vector.tensor_tensor(xs[:, b0:b1, :], xs[:, b0:b1, :], qn[:, b0:b1, :], ALU.add))
                settle()
                layernorm(qn, xs, b0, b1, z3_ready)

            def route(g):
                dve.wait_ge(route_ps, g + 1)
                logit = rt[:, 0, :, :]
                own(nc.vector.tensor_copy(logit, ps[:, 7, 0:GB * EXP].rearrange("p (b e) -> p b e", b=GB)))
                settle()
                for b in range(GB):
                    own(nc.vector.max(rt[:, 3, b, :], rt[:, 0, b, :]))
                settle()
                top1 = rt[:, 3, :, 0:1].to_broadcast([128, GB, EXP])
                top2 = rt[:, 3, :, 1:2].to_broadcast([128, GB, EXP])
                nc.vector.tensor_tensor(rt[:, 1, :, :], logit, top1, ALU.subtract).then_inc(route_sub, 1)
                own(nc.vector.tensor_tensor(rt[:, 4, :, :], logit, top2, ALU.is_gt))
                own(nc.vector.tensor_tensor(rt[:, 5, :, :], logit, top2, ALU.is_equal))
                settle()
                own(nc.vector.tensor_reduce(rt[:, 8, :, 0], rt[:, 4, :, :], AX, ALU.add))
                own(nc.vector.tensor_copy(rt[:, 6, :, :], rt[:, 5, :, :]))
                settle()
                a, b_ = 6, 7
                for d in (1, 2, 4):
                    own(nc.vector.tensor_copy(rt[:, b_, :, 0:d], rt[:, a, :, 0:d]))
                    own(nc.vector.tensor_tensor(rt[:, b_, :, d:EXP], rt[:, a, :, d:EXP],
                                                rt[:, a, :, 0:EXP - d], ALU.add))
                    settle()
                    a, b_ = b_, a
                own(nc.vector.tensor_tensor(rt[:, b_, :, :], rt[:, a, :, :],
                                            rt[:, 8, :, 0:1].to_broadcast([128, GB, EXP]), ALU.add))
                settle()
                own(nc.vector.tensor_scalar(rt[:, a, :, :], rt[:, b_, :, :], 2.0, None, ALU.is_le))
                settle()
                own(nc.vector.tensor_tensor(rt[:, 5, :, :], rt[:, 5, :, :], rt[:, a, :, :], ALU.mult))
                settle()
                own(nc.vector.tensor_tensor(rt[:, 4, :, :], rt[:, 4, :, :], rt[:, 5, :, :], ALU.add))
                settle()
                dve.wait_ge(route_exp, g + 1)
                own(nc.vector.tensor_tensor(rt[:, 9, :, :], rt[:, 2, :, :], rt[:, 4, :, :], ALU.mult))
                settle()
                own(nc.vector.tensor_reduce(rt[:, 10, :, 0], rt[:, 9, :, :], AX, ALU.add))
                settle()
                own(nc.vector.reciprocal(rt[:, 11, :, 0], rt[:, 10, :, 0]))
                settle()
                own(nc.vector.tensor_tensor(pw[:, g * GB:(g + 1) * GB, :], rt[:, 9, :, :],
                                            rt[:, 11, :, 0:1].to_broadcast([128, GB, EXP]), ALU.mult))
                settle()

            for g in range(NG):
                route(g)
                for i in range(HCH):
                    u = g * HCH + i
                    dve.wait_ge(act_ready, u + 1)
                    if i == 0 and g:
                        dve.wait_ge(down_ps, g * GB * 3)
                    nc.vector.tensor_tensor(hid[:, i, :], gact[:, u % 4, :], ps[:, (u % 2) * 2 + 1, :],
                                            ALU.mult).then_inc(hid_ready, 1)
                for bl in range(GB):
                    b = g * GB + bl
                    for m in range(3):
                        u = b * 3 + m
                        bank = 4 + u % 3
                        dve.wait_ge(down_ps, u + 1)
                        if m == 0:
                            ins = nc.vector.tensor_tensor(y3[:, b, :], ps[:, bank, 0:C], xs[:, b, :], ALU.add)
                            ins.then_inc(down_used, 1)
                            dve.wait_ge(down_used, u + 1)
                        else:
                            for e in range(4):
                                ex = expert(m, e)
                                ins = nc.vector.scalar_tensor_tensor(
                                    y3[:, b, :], ps[:, bank, e * C:(e + 1) * C], pw[:, b, ex:ex + 1],
                                    y3[:, b, :], ALU.mult, ALU.add)
                                if e == 3:
                                    ins.then_inc(down_used, 1)
                                    dve.wait_ge(down_used, u + 1)
                                else:
                                    own(ins)
                                    settle()

        @block.tensor
        def _(pe):
            pe.wait_ge(ld["consts"], 32)
            for b in range(B):
                pe.wait_ge(z_ready, b + 1)
                ins = nc.tensor.transpose(ps[:, b // GB, (b % GB) * T:(b % GB + 1) * T], z[:, b, :], ident[:, :])
                if b % GB == GB - 1:
                    ins.then_inc(zT_ps, 1)
            pe.wait_ge(ld["wqkvb"], 16)
            for bank, m in ((2, 1), (6, 2), (0, 0), (4, 3)):
                for h in range(2):
                    pe.wait_ge(nT_ready, 2 if bank == 0 else h + 1)
                    nc.tensor.matmul(ps[:, bank + h, :], wqkvb_s[:, m * C:(m + 1) * C], nT[:, h * GT:(h + 1) * GT],
                                     start=True, stop=True).then_inc(proj_ps, 1)
                if m == 2:
                    for h in range(2):
                        pe.wait_ge(proj_ev, h + 1)
                        nc.tensor.matmul(ps[:, 2 + h, :], same_head[:, :], sq[:, h * GT:(h + 1) * GT],
                                         start=True, stop=True).then_inc(norm_ps, 1)
            pe.wait_ge(ld["sel"], 16)
            pe.wait_ge(kn_ready, 2)
            pe.wait_ge(proj_ev, 8)

            def spread(c):
                for u in range(4):
                    src = kT if u < 2 else qT
                    n = 4 * c + u
                    if n >= 2:
                        pe.wait_ge(spread_ev, n - 1)
                    for j in range(4):
                        ins = nc.tensor.matmul(
                            ps[:, 2 * (u % 2) + j // 2, (j % 2) * 256:(j % 2) * 256 + 256],
                            sel[:, 4 * (u % 2) + j, :],
                            (src[:, 0:B * T]).rearrange("p (b t) -> p b t", b=B)[:, :, c * CH:(c + 1) * CH],
                            start=True, stop=True)
                    ins.then_inc(spread_ps, 1)

            def ctx_project(i):
                kind, a, h = CTX_UNITS[i]
                if i >= 3:
                    pe.wait_ge(ctxp_ev, i - 2)
                if kind == "k":
                    nc.tensor.matmul(ps[:, 4 + i % 3, 0:GB * J], Wk_s[:, h * 128:(h + 1) * 128],
                                     ctxT_s[:, a * GB:(a + 1) * GB, :],
                                     start=True, stop=True).then_inc(ctxp_ps, 1)
                else:
                    nc.tensor.matmul(ps[0:J, 4 + i % 3, :], ctxT_s[:, a, :], Wv_s[:, h * BANK:(h + 1) * BANK],
                                     start=True, stop=True).then_inc(ctxp_ps, 1)

            def attend(c):
                pe.wait_ge(scan_done, c + 1)
                if c >= 1:
                    pe.wait_ge(att_ev, c)
                for j in range(DH):
                    ins = nc.tensor.matmul(ps[:, 7, (c % 2) * 256:(c % 2) * 256 + 256], wout_s,
                                           qx[:, c % 2, :, :, j].rearrange("p t b -> p b t"),
                                           start=(j == 0), stop=(j == DH - 1))
                ins.then_inc(att_ps, 1)

            spread(0)
            pe.wait_ge(ld["Wr"], 16)
            pe.wait_ge(small_ready, 1)
            for n in range(XH):
                r = 64 * (n % 2)
                ins = nc.tensor.matmul(ps[:, 6 + n % 2, n:n + 1], WrT_s[r:r + 64, n // 2, :], small[r:r + 64, 3:4],
                                       start=True, stop=True)
            ins.then_inc(relb_ps, 1)
            spread(1)
            pe.wait_ge(ld["ctx"], 16)
            pe.wait_ge(ld["Wk"], 16)
            pe.wait_ge(ld["Wv"], 16)
            pe.wait_ge(ld["wout"], 16)
            pe.wait_ge(relb_ready, 2)
            for i in range(CTX_SPLIT):
                ctx_project(i)
            attend(0)
            spread(2)
            for i in range(CTX_SPLIT, len(CTX_UNITS)):
                ctx_project(i)
            attend(1)
            spread(3)
            attend(2)
            attend(3)
            pe.wait_ge(att_ev, 4)
            pe.wait_ge(spread_ev, 4 * NC)
            for b in range(B):
                ins = nc.tensor.transpose(ps[:, b // GB, (b % GB) * C:(b % GB + 1) * C],
                                          attT[:, b * T:(b + 1) * T], ident[:, :])
                if b % GB == GB - 1:
                    ins.then_inc(x2_ps, 1)

            for b in range(B):
                pe.wait_ge(qn_ready, b + 1)
                ins = nc.tensor.transpose(ps[:, 2 + b // GB, (b % GB) * T:(b % GB + 1) * T], qn[:, b, :],
                                          ident[:, :])
                if b % GB == GB - 1:
                    ins.then_inc(qnT_ps, 1)
            pe.wait_ge(ld["Wq"], 16)
            pe.wait_ge(ld["Wo"], 16)
            pe.wait_ge(ld["tail"], 48)

            def scores(k):
                b, q4 = k // 4, k % 4
                bl = b % GB
                if k % (GB * 4) >= 2:
                    pe.wait_ge(p_ready, k - 1)
                for h in range(4):
                    n = head(q4, h)
                    r = 64 * (n % 2)
                    nc.tensor.matmul(ps[:, k % 2, h * J:(h + 1) * J], relT[:, bl * XH + n, :],
                                     ident[0:J, 0:J], is_transpose=True, start=True, stop=False)
                    ins = nc.tensor.matmul(ps[:, k % 2, h * J:(h + 1) * J],
                                           hqu[r:r + 64, n // 2, bl * T:(bl + 1) * T],
                                           hk[r:r + 64, n // 2, b, :], start=False, stop=True)
                ins.then_inc(s_ps, 1)

            def turn(k):
                pe.wait_ge(p_ready, k + 1)
                if k >= 2:
                    pe.wait_ge(pT_ready, k - 1)
                for h in range(4):
                    ins = nc.tensor.transpose(ps[0:J, 2 + k % 2, h * T:(h + 1) * T], pbuf[:, k % 4, h, :],
                                              ident[:, :])
                ins.then_inc(pT_ps, 1)

            def values(k):
                b, q4 = k // 4, k % 4
                pe.wait_ge(pT_ready, k + 1)
                if q4 == 0 and b >= 1:
                    pe.wait_ge(osc_ready, 2 * b)
                for h in range(4):
                    n = head(q4, h)
                    ins = nc.tensor.matmul(ps[:, 4 + n // 8, (n % 8) * DK:(n % 8 + 1) * DK],
                                           pT[:, k % 4, h, :], hv[:, b, n * DK:(n + 1) * DK],
                                           start=True, stop=True)
                ins.then_inc(o_ps, 1)

            def gates(g):
                if g:
                    pe.wait_ge(y_ready, g * GB)
                for bl in range(GB):
                    b = g * GB + bl
                    ins = nc.tensor.matmul(ps[:, 7, 128 + bl * XH:128 + (bl + 1) * XH],
                                           qT[:, b * T:(b + 1) * T], hw_s[:, :], start=True, stop=True)
                ins.then_inc(gate_ps, 1)

            def outputs(b):
                for h in range(2):
                    pe.wait_ge(osc_ready, 2 * b + h + 1)
                    if 2 * b + h >= 1:
                        pe.wait_ge(oT_ready, 2 * b + h)
                    for p in range(4):
                        ins = nc.tensor.transpose(ps[:, 6, p * T:(p + 1) * T],
                                                  osc[:, (4 * h + p) * 128:(4 * h + p + 1) * 128], ident[:, :])
                    ins.then_inc(oT_ps, 1)
                pe.wait_ge(oT_ready, 2 * b + 2)
                pe.wait_ge(gate_t, b // GB + 1)
                if b >= 1:
                    pe.wait_ge(y_ready, b)
                for p in range(PAIRS):
                    ins = nc.tensor.matmul(ps[:, 7, 0:C], oT[:, p, :], Wo_s[:, p, :],
                                           start=(p == 0), stop=(p == PAIRS - 1))
                ins.then_inc(y_ps, 1)

            for g in range(NG):
                first, last = g * GB * 4, (g + 1) * GB * 4
                pe.wait_ge(qT_ready, 2)
                if g:
                    pe.wait_ge(p_ready, first)
                    pe.wait_ge(pT_ready, first)
                for p in range(PAIRS):
                    if p >= 4:
                        pe.wait_ge(hq_ev, g * PAIRS + p - 3)
                    nc.tensor.matmul(ps[:, p % 4, :], Wq_s[:, p * 128:(p + 1) * 128], qT[:, g * GT:(g + 1) * GT],
                                     start=True, stop=True).then_inc(hq_ps, 1)
                for n in range(XH):
                    r = 64 * (n % 2)
                    pe.wait_ge(hq_ev, g * PAIRS + PAIRS)
                    if n >= 4:
                        pe.wait_ge(w_ev, g * XH + n - 3)
                    nc.tensor.matmul(ps[:, n % 4, :], WrT_s[r:r + 64, n // 2, :], hqu[r:r + 64, n // 2, :],
                                     start=True, stop=True).then_inc(w_ps, 1)
                pe.wait_ge(w_ev, (g + 1) * XH)
                for i in range(T):
                    if i % 8 == 0 and i >= 32:
                        pe.wait_ge(rel_ev, g * (T // 8) + i // 8 - 3)
                    ins = nc.tensor.matmul(ps[0:J, (i // 8) % 4, (i % 8) * 64:(i % 8 + 1) * 64],
                                           rel_s[:, T - 1 - i:T - 1 - i + J], wrel[:, i, :],
                                           start=True, stop=True)
                    if i % 8 == 7:
                        ins.then_inc(rel_ps, 1)
                gates(g)
                pe.wait_ge(rel_ev, (g + 1) * (T // 8))
                for k in range(first, last + 3):
                    if k < last:
                        scores(k)
                    if first <= k - 1 < last:
                        turn(k - 1)
                    if first <= k - 2 < last:
                        values(k - 2)
                        if (k - 2) % 4 == 3:
                            outputs((k - 2) // 4)

            for b in range(B):
                g = b // GB
                pe.wait_ge(z3_ready, b + 1)
                ins = nc.tensor.transpose(ps[:, 4 + g, (b % GB) * T:(b % GB + 1) * T], qn[:, b, :], ident[:, :])
                if b % GB == GB - 1:
                    ins.then_inc(z3T_ps, 1)
            pe.wait_ge(ld["moe"], 48)
            for g in range(NG):
                pe.wait_ge(z3T_ready, g + 1)
                if g:
                    pe.wait_ge(route_sub, g)
                for bl in range(GB):
                    b = g * GB + bl
                    ins = nc.tensor.matmul(ps[:, 7, bl * EXP:(bl + 1) * EXP], qT[:, b * T:(b + 1) * T], Wg_s[:, :],
                                           start=True, stop=True)
                ins.then_inc(route_ps, 1)
                for i in range(HCH):
                    u = g * HCH + i
                    if u >= 2:
                        pe.wait_ge(hid_ready, u - 1)
                    nc.tensor.matmul(ps[:, (u % 2) * 2, :], W1_s[:, i, :], qT[:, g * GT:(g + 1) * GT],
                                     start=True, stop=True)
                    nc.tensor.matmul(ps[:, (u % 2) * 2 + 1, :], W2_s[:, i, :], qT[:, g * GT:(g + 1) * GT],
                                     start=True, stop=True).then_inc(up_ps, 1)
                pe.wait_ge(hid_ready, (g + 1) * HCH)
                pe.wait_ge(z3T_ready, 2)
                for bl in range(GB):
                    b = g * GB + bl
                    tok = slice(bl * T, (bl + 1) * T)
                    for m in range(3):
                        u = b * 3 + m
                        bank = 4 + u % 3
                        if u >= 3:
                            pe.wait_ge(down_used, u - 2)
                        if m == 0:
                            for s in range(3):
                                r = 128 if s < 2 else SHID - 256
                                ins = nc.tensor.matmul(ps[:, bank, 0:C], hid[0:r, 12 + s, tok],
                                                       W3_s[0:r, 12 + s, :], start=(s == 0), stop=(s == 2))
                        else:
                            for e in range(4):
                                ex = expert(m, e)
                                r = 64 * (ex % 2)
                                nc.tensor.matmul(ps[:, bank, e * C:(e + 1) * C], hid[:, ex, tok],
                                                 W3_s[:, ex, :], start=True, stop=False)
                                ins = nc.tensor.matmul(ps[:, bank, e * C:(e + 1) * C],
                                                       hid[r:r + REST, EXP + ex // 2, tok],
                                                       W3_s[r:r + REST, EXP + ex // 2, :],
                                                       start=False, stop=True)
                        ins.then_inc(down_ps, 1)


def _layout(i):
    import numpy as np
    a = {k: np.asarray(v) for k, v in i.items()}

    def heads(w):
        return np.ascontiguousarray(w.reshape(C, DK, XH).transpose(0, 2, 1).reshape(C, XH * DK))

    def by_pair(w):
        return np.ascontiguousarray(w.reshape(DK, PAIRS, 2, C).transpose(2, 0, 1, 3).reshape(128, PAIRS, C))

    freq = (1.0 / 10000.0 ** (np.arange(0, C, 2, dtype=np.float32) / np.float32(C))).astype(np.float32)
    pos = np.arange(T - 1, -J, -1).astype(np.float32)
    ang = pos[:, None] * freq[None, :]
    emb = np.stack([np.sin(ang) * np.float32(0.1 * C), np.cos(ang) * np.float32(0.1 * C)], -1)
    rel = np.ascontiguousarray(emb.reshape(NREL, C).T.astype(np.float32))

    p = np.arange(128)
    ident = (p[:, None] == p[None, :]).astype(np.float32)
    same = (p[:, None] // DH == p[None, :] // DH).astype(np.float32)
    sel = np.stack([same * (p[:, None] % DH == j) for j in range(DH)], 1).astype(np.float32)
    consts = np.concatenate([ident, same, sel.reshape(128, DH * 128)], 1)

    def up(w, ws):
        o = np.zeros((C, HCH, 128), np.float32)
        o[:, :EXP] = w[:, :, :128].transpose(1, 0, 2)
        for e in range(EXP):
            r = 64 * (e % 2)
            o[:, EXP + e // 2, r:r + REST] = w[e, :, 128:]
        o[:, 12] = ws[:, 0:128]
        o[:, 13] = ws[:, 128:256]
        o[:, 14, :SHID - 256] = ws[:, 256:]
        return o

    w3 = np.zeros((128, HCH, C), np.float32)
    w3[:, :EXP] = a["L0_ffn_W3"][:, :128].transpose(1, 0, 2)
    for e in range(EXP):
        r = 64 * (e % 2)
        w3[r:r + REST, EXP + e // 2] = a["L0_ffn_W3"][e, 128:]
    w3[:, 12] = a["L0_ffn_Ws3"][0:128]
    w3[:, 13] = a["L0_ffn_Ws3"][128:256]
    w3[:SHID - 256, 14] = a["L0_ffn_Ws3"][256:]

    bq = a["L0_attn_b_qkvb"].reshape(4, C)
    twice = lambda v: np.concatenate([v, v])
    cols = np.stack([a["L0_attn_ln_g"], a["L0_attn_ln_b"], bq[0], bq[1], bq[2], bq[3],
                     twice(a["L0_xattn_ub_w"]), twice(a["L0_xattn_vb_w"])], 1)
    rows = np.stack([a["L0_attn_b_out"], a["L0_xattn_ln_g"], a["L0_xattn_ln_b"]])
    return {
        "x": a["x"],
        "ctxT": np.ascontiguousarray(a["ctx_1024"].transpose(2, 0, 1)),
        "maskT": np.ascontiguousarray(a["mask_BxSxS2_bf0"].transpose(2, 0, 1)),
        "w_qkvb": a["L0_attn_w_qkvb"], "w_out": a["L0_attn_w_out"], "cols": cols, "rows": rows,
        "consts": consts,
        "Wq": heads(a["L0_xattn_Wq"]), "Wk": heads(a["L0_xattn_Wk"]), "Wv": heads(a["L0_xattn_Wv"]),
        "WrT": by_pair(np.ascontiguousarray(a["L0_xattn_Wr"].T)),
        "Wo": by_pair(a["L0_xattn_Wo"]), "head_w": a["L0_xattn_head_w"], "rel_tab": rel,
        "Wg": a["L0_ffn_Wg"], "W1": up(a["L0_ffn_W1"], a["L0_ffn_Ws1"]),
        "W2": up(a["L0_ffn_W2"], a["L0_ffn_Ws2"]), "W3": w3,
    }


def kernel(**inputs):
    import numpy as np
    import concourse.bacc as bacc
    from concourse import mybir as mb
    from concourse.bass_utils import run_bass_kernel_spmd

    laid = _layout(inputs)
    nc = bacc.Bacc("TRN2", target_bir_lowering=False, num_devices=1)
    arrays, args = {}, []
    for name, a in laid.items():
        a = np.ascontiguousarray(a)
        arrays[f"in_{name}"] = a
        args.append(nc.dram_tensor(f"in_{name}", a.shape, mb.dt.from_np(a.dtype), kind="ExternalInput").ap())
    args.append(nc.dram_tensor("out", (B, T, C), mb.dt.float32, kind="ExternalOutput").ap())
    layer(nc, *args)
    r = run_bass_kernel_spmd(nc, [arrays], core_ids=[0])
    return r.results[0]["out"]
```

```python
import concourse.bass as bass
from concourse import mybir
from contextlib import ExitStack

B, T, C = 8, 128, 128
NH, DH = 16, 8
CH = 32
NC = T // CH
J = 120
XH, DK = 16, 64
PAIRS = XH // 2
GB = 4
NG = B // GB
GT = GB * T
NREL = T + J - 1
EXP, HID = 8, 176
REST = HID - 128
SHID = 352
HCH = EXP + EXP // 2 + 3
BANK = 512
LN_EPS = 1e-5
NORM_EPS = 1e-6
SCALE = float(C) ** -0.5
NEG = -1.0e9


def layer(nc, x, ctxT, maskT, w_qkvb, w_out, cols, rows, consts, Wq, Wk, Wv, WrT, Wo, head_w, rel_tab,
          Wg, W1, W2, W3, out):
    fp32 = mybir.dt.float32
    u8 = mybir.dt.uint8
    ALU = mybir.AluOpType
    ACT = mybir.ActivationFunctionType
    AX = mybir.AxisListType.X

    ctx = ExitStack()
    with ctx:
        def sb(name, shape, dt=fp32):
            return ctx.enter_context(nc.sbuf_tensor(name, shape, dt))

        def sem(name):
            return ctx.enter_context(nc.semaphore(name))

        hk = sb("hk", [128, PAIRS, B, J])
        hv = sb("hv", [J, B, XH * DK])
        xs = sb("xs", [128, B, C])
        qn = sb("qn", [128, B, C])
        qT = sb("qT", [128, B * T])
        Wq_s = sb("Wq_s", [128, XH * DK])
        WrT_s = sb("WrT_s", [128, PAIRS, C])
        Wo_s = sb("Wo_s", [128, PAIRS, C])
        rel_s = sb("rel_s", [128, NREL])
        ident = sb("ident", [128, 128])
        same_head = sb("same_head", [128, 128])
        hw_s = sb("hw_s", [128, XH])
        Wg_s = sb("Wg_s", [128, EXP])
        rows_s = sb("rows_s", [128, 3, C])
        cols_s = sb("cols_s", [128, 8])
        maskadd = sb("maskadd", [J, B, T])
        mask_s = sb("mask_s", [J, B, T], u8)
        small = sb("small", [128, 16])
        relb = sb("relb", [128, XH])
        st = sb("st", [128, B, 6])
        mv = sb("mv", [128, B, 2])
        rs = sb("rs", [128, B])
        var = sb("var", [128, B])
        neg_half = sb("neg_half", [128, B])
        nmax = sb("nmax", [128, XH * B])
        rsum = sb("rsum", [128, XH * B])
        gate = sb("gate", [128, GB, XH])
        rden = sb("rden", [128, XH])
        rt = sb("rt", [128, 12, GB, EXP])
        pw = sb("pw", [128, B, EXP])

        REGION = 26624
        region = sb("region", [128, REGION])
        at = [0]

        def cut(*shape, p=128):
            n = 1
            for s in shape:
                n *= s
            assert at[0] + n <= REGION, at[0] + n
            a = region[0:p, at[0]:at[0] + n]
            at[0] += n
            names = "abcd"[:len(shape)]
            if len(shape) == 1:
                return a
            return a.rearrange(f"p ({' '.join(names)}) -> p {' '.join(names)}",
                               **dict(zip(names, shape)))

        kx = cut(2, CH, B, DH + 1)
        mx = cut(2, CH, B, DH + 1)
        qx = cut(2, CH, B, DH)
        hist = cut(CH, B, DH + 1)
        xn = cut(B, C)
        z = cut(B, C)
        nT = cut(B * T)
        kT = cut(B * T)
        vT = cut(B * T)
        beta = cut(B * T)
        sel = cut(DH, 128)
        wqkvb_s = cut(4 * C)
        wout_s = cut(C)
        Wk_s = cut(XH * DK)
        Wv_s = cut(XH * DK)
        ctxT_s = cut(B, J)
        sq = z.rearrange("p b t -> p (b t)")
        attT = sq
        kk = xn.rearrange("p b t -> p (b t)")
        gT = kk
        at[0] = 0
        wrel = cut(T, GB * XH)
        relT = cut(GB * XH, T, p=J)
        hqu = cut(PAIRS, GT)
        pbuf = cut(4, 4, J)
        pT = cut(4, 4, T, p=J)
        osc = cut(XH * DK)
        oT = cut(PAIRS, T)
        at[0] = 0
        W1_s = cut(HCH, 128)
        W2_s = cut(HCH, 128)
        W3_s = cut(HCH, C)
        hid = cut(HCH, GT)
        gact = cut(4, GT)
        y3 = cut(B, C)

        fT = sb("fT", [128, B * T])
        terms = sb("terms", [128, 2, B, 2 * DH + 2])
        upd = sb("upd", [128, 2, B])

        ps = ctx.enter_context(nc.psum_tensor("ps", [128, 8, BANK], fp32))

        ld = {n: sem("ld_" + n) for n in
              ["x0", "x1", "cols", "rows", "ident", "same", "sel", "wqkvb", "wout", "ctx", "Wk", "Wv", "Wq",
               "Wr", "Wo", "tail", "mask", "moe"]}
        var_ready = sem("var_ready")
        rs_ready = sem("rs_ready")
        xn_ready = sem("xn_ready")
        z_ready = sem("z_ready")
        zT_ps = sem("zT_ps")
        nT_ready = sem("nT_ready")
        k_ps = sem("k_ps")
        kT_ready = sem("kT_ready")
        sq_ready = sem("sq_ready")
        norm_ps = sem("norm_ps")
        norm_ready = sem("norm_ready")
        small_ready = sem("small_ready")
        beta_ps = sem("beta_ps")
        beta_ready = sem("beta_ready")
        v_ps = sem("v_ps")
        v_ready = sem("v_ready")
        q_ps = sem("q_ps")
        q_ready = sem("q_ready")
        kk_ready = sem("kk_ready")
        kk_ps = sem("kk_ps")
        share_ready = sem("share_ready")
        values_ready = sem("values_ready")
        spread_ps = sem("spread_ps")
        spread_ev = sem("spread_ev")
        kx_ready = sem("kx_ready")
        scan_step = sem("scan_step")
        scan_done = sem("scan_done")
        att_ps = sem("att_ps")
        att_ev = sem("att_ev")
        ctxp_ps = sem("ctxp_ps")
        ctxp_ev = sem("ctxp_ev")
        base_ready = sem("base_ready")
        mask_ready = sem("mask_ready")
        relb_ps = sem("relb_ps")
        relb_ready = sem("relb_ready")
        x2_ps = sem("x2_ps")
        qn_ready = sem("qn_ready")
        qnT_ps = sem("qnT_ps")
        qT_ready = sem("qT_ready")
        hq_ps = sem("hq_ps")
        hq_ev = sem("hq_ev")
        w_ps = sem("w_ps")
        w_ev = sem("w_ev")
        rel_ps = sem("rel_ps")
        rel_ev = sem("rel_ev")
        s_ps = sem("s_ps")
        max_ready = sem("max_ready")
        p_ready = sem("p_ready")
        pT_ps = sem("pT_ps")
        pT_ready = sem("pT_ready")
        o_ps = sem("o_ps")
        gate_ps = sem("gate_ps")
        gate_t = sem("gate_t")
        osc_ready = sem("osc_ready")
        oT_ps = sem("oT_ps")
        oT_ready = sem("oT_ready")
        y_ps = sem("y_ps")
        y_ready = sem("y_ready")
        z3_ready = sem("z3_ready")
        z3T_ps = sem("z3T_ps")
        z3T_ready = sem("z3T_ready")
        route_ps = sem("route_ps")
        logits_ready = sem("logits_ready")
        route_sub = sem("route_sub")
        route_exp = sem("route_exp")
        up_ps = sem("up_ps")
        act_ready = sem("act_ready")
        hid_ready = sem("hid_ready")
        down_ps = sem("down_ps")
        down_used = sem("down_used")
        stored = sem("stored")
        vec = sem("vec")
        pool_own = sem("pool_own")

        CTX_UNITS = [("k", g, p) for g in range(NG) for p in range(PAIRS)] + \
                    [("v", b, h) for b in range(B) for h in range(2)]
        CTX_SPLIT = 16
        NU = GB * 4
        TURN, VALUES = 2, 3
        STEPS = NU + 7
        SCALE_AT, OT_AT, Y_AT, SUM_AT = (5, 7), (7, 8), 9, 10

        def due(i, at):
            return (i - at) // 4 if i >= at and (i - at) % 4 == 0 and (i - at) // 4 < GB else None

        def hq_bank(g, p):
            return 4 + p % 4 if g == 0 else p % 3

        def head(q4, h):
            return 8 * (q4 // 2) + 2 * h + q4 % 2

        def expert(m, e):
            return 2 * e + m - 1

        HQ_EARLY = 4
        UP_FROM = NU + 2
        UP_EARLY = STEPS - UP_FROM

        block = ctx.enter_context(nc.Block())

        @block.sync
        def _(sp):
            for h in range(2):
                sp.dma_start(xs[:, h * GB:(h + 1) * GB, :],
                             x[h * GB:(h + 1) * GB, :, :].rearrange("b t c -> t b c")).then_inc(ld[f"x{h}"], 16)
            sp.dma_start(ident[:, :], consts[:, 0:128]).then_inc(ld["ident"], 16)
            sp.dma_start(wqkvb_s, w_qkvb).then_inc(ld["wqkvb"], 16)
            sp.dma_start(same_head[:, :], consts[:, 128:256]).then_inc(ld["same"], 16)
            sp.dma_start(sel.rearrange("p a b -> p (a b)"), consts[:, 256:256 + DH * 128]).then_inc(ld["sel"], 16)
            sp.dma_start(rows_s[:, :, :].rearrange("p a c -> p (a c)"),
                         rows.rearrange("a c -> (a c)").partition_broadcast(128)).then_inc(ld["rows"], 16)
            sp.dma_start(WrT_s[:, :, :], WrT).then_inc(ld["Wr"], 16)
            sp.dma_start(ctxT_s, ctxT).then_inc(ld["ctx"], 16)
            sp.dma_start(Wk_s, Wk).then_inc(ld["Wk"], 16)
            sp.dma_start(Wv_s, Wv).then_inc(ld["Wv"], 16)
            sp.dma_start(wout_s, w_out).then_inc(ld["wout"], 16)
            sp.dma_start(mask_s[:, :, :], maskT).then_inc(ld["mask"], 16)
            sp.dma_start(Wq_s[:, :], Wq).then_inc(ld["Wq"], 16)
            sp.dma_start(rel_s[:, :], rel_tab).then_inc(ld["tail"], 16)
            sp.dma_start(hw_s[:, :], head_w).then_inc(ld["tail"], 16)
            sp.dma_start(Wg_s[:, :], Wg).then_inc(ld["tail"], 16)
            sp.dma_start(Wo_s[:, :, :], Wo).then_inc(ld["Wo"], 16)
            sp.wait_ge(rel_ps, NG * T // 8)
            sp.dma_start(W1_s, W1).then_inc(ld["moe"], 16)
            sp.dma_start(W2_s, W2).then_inc(ld["moe"], 16)
            sp.dma_start(W3_s, W3).then_inc(ld["moe"], 16)
            for b in range(B):
                sp.wait_ge(down_used, 3 * (b + 1))
                sp.dma_start(out[b, :, :], y3[:, b, :]).then_inc(stored, 16)
            sp.wait_ge(stored, 16 * B)

        @block.gpsimd
        def _(pool):
            nc.gpsimd.memset(neg_half[:, :], -0.5).then_inc(pool_own, 1)
            pool.wait_ge(pool_own, 1)

            def inverse_roots(i, g):
                pool.wait_ge(var_ready, i + 1)
                nc.gpsimd.tensor_tensor(rs[:, g * GB:(g + 1) * GB], var[:, g * GB:(g + 1) * GB],
                                        neg_half[:, 0:GB], ALU.pow).then_inc(rs_ready, 1)

            for i in range(4):
                inverse_roots(i, i % 2)
            pool.wait_ge(xn_ready, B)
            nc.gpsimd.tensor_tensor(xs[:, :, :], xs[:, :, :], xn, ALU.add).then_inc(pool_own, 1)
            pool.wait_ge(pool_own, 2)
            pool.wait_ge(z_ready, B)
            pool.wait_ge(kT_ready, 2)
            kv = kT.rearrange("p (b t) -> p b t", b=B)
            kkv = kk.rearrange("p (b t) -> p b t", b=B)
            nc.gpsimd.memset(kkv[:, :, T - 1:T], 0.0).then_inc(kk_ready, 1)
            nc.gpsimd.tensor_tensor(kkv[:, :, 0:T - 1], kv[:, :, 0:T - 1], kv[:, :, 1:T],
                                    ALU.mult).then_inc(kk_ready, 1)
            pool.wait_ge(ld["rows"], 16)
            nc.gpsimd.tensor_tensor(xs[:, :, :], xs[:, :, :],
                                    rows_s[:, 0:1, :].to_broadcast([128, B, C]), ALU.add).then_inc(base_ready, 1)
            pool.wait_ge(ld["mask"], 16)
            nc.gpsimd.tensor_scalar(maskadd[:, :, :], mask_s[:, :, :], NEG, None, ALU.mult).then_inc(mask_ready, 1)
            for i in range(4, 6):
                inverse_roots(i, i % 2)
            for g in range(NG):
                inverse_roots(6 + 2 * g, g)
                inverse_roots(7 + 2 * g, g)

        @block.scalar
        def _(act):
            act.dma_start(cols_s[:, :], cols).then_inc(ld["cols"], 16)
            act.wait_ge(ld["cols"], 16)
            for h in range(2):
                act.wait_ge(zT_ps, h + 1)
                nc.scalar.activation(nT[:, h * GT:(h + 1) * GT], ps[:, h, :], ACT.Identity,
                                     scale=cols_s[:, 0:1], bias=cols_s[:, 1:2]).then_inc(nT_ready, 1)
            for h in range(2):
                act.wait_ge(k_ps, h + 1)
                nc.scalar.activation(sq[:, h * GT:(h + 1) * GT], ps[:, 2 + h, :], ACT.Square,
                                     bias=cols_s[:, 3:4]).then_inc(sq_ready, 1)
                nc.scalar.activation(kT[:, h * GT:(h + 1) * GT], ps[:, 2 + h, :], ACT.Identity,
                                     bias=cols_s[:, 3:4]).then_inc(kT_ready, 1)
            for h in range(2):
                act.wait_ge(norm_ps, h + 1)
                nc.scalar.activation(sq[:, h * GT:(h + 1) * GT], ps[:, 4 + h, :], ACT.Sqrt).then_inc(norm_ready, 1)

            def spread_out(dst, c, u):
                act.wait_ge(spread_ps, 4 * c + u + 1)
                for s in range(2):
                    j = 4 * (u % 2) + 2 * s
                    ins = nc.scalar.activation(
                        dst[:, c % 2, :, :, j:j + 2].rearrange("p t b j -> p j b t"),
                        ps[:, 2 * (u % 2) + s, :].rearrange("p (j b t) -> p j b t", j=2, b=B), ACT.Copy)
                return ins.then_inc(spread_ev, 1)

            def last_column(dst, src, c):
                return nc.scalar.activation(dst[:, c % 2, :, :, DH].rearrange("p t b -> p b t"),
                                            src.rearrange("p (b t) -> p b t", b=B)[:, :, c * CH:(c + 1) * CH],
                                            ACT.Copy)

            def chunk_out(c):
                if c >= 2:
                    act.wait_ge(scan_done, c - 1)
                spread_out(kx, c, 0)
                spread_out(kx, c, 1)
                last_column(kx, gT, c)
                last_column(mx, vT, c).then_inc(kx_ready, 1)
                if c >= 2:
                    act.wait_ge(att_ps, c - 1)
                spread_out(qx, c, 2)
                spread_out(qx, c, 3)

            def ctx_out(i):
                kind, a, h = CTX_UNITS[i]
                act.wait_ge(ctxp_ps, i + 1)
                if kind == "k":
                    nc.scalar.activation(hk[:, h, a * GB:(a + 1) * GB, :],
                                         ps[:, 4 + i % 3, 0:GB * J].rearrange("p (b j) -> p b j", b=GB),
                                         ACT.Copy).then_inc(ctxp_ev, 1)
                else:
                    nc.scalar.activation(hv[:, a, h * BANK:(h + 1) * BANK], ps[0:J, 4 + i % 3, :],
                                         ACT.Copy).then_inc(ctxp_ev, 1)

            def att_out(c):
                act.wait_ge(att_ps, c + 1)
                nc.scalar.activation(attT.rearrange("p (b t) -> p b t", b=B)[:, :, c * CH:(c + 1) * CH],
                                     ps[:, 7, (c % 2) * 256:(c % 2) * 256 + 256]
                                     .rearrange("p (b t) -> p b t", b=B), ACT.Copy).then_inc(att_ev, 1)

            spread_out(kx, 0, 0)
            act.wait_ge(small_ready, 1)
            for h in range(2):
                act.wait_ge(beta_ps, h + 1)
                nc.scalar.activation(beta[:, h * GT:(h + 1) * GT], ps[:, 6 + h, :], ACT.Tanh,
                                     bias=small[:, 0:1], scale=0.5).then_inc(beta_ready, 1)
            spread_out(kx, 0, 1)
            for h in range(2):
                act.wait_ge(v_ps, h + 1)
                nc.scalar.activation(vT[:, h * GT:(h + 1) * GT], ps[:, h, :], ACT.Identity,
                                     bias=cols_s[:, 4:5]).then_inc(v_ready, 1)
            act.wait_ge(share_ready, 2)
            last_column(kx, gT, 0)
            act.wait_ge(values_ready, 1)
            last_column(mx, vT, 0).then_inc(kx_ready, 1)
            for h in range(2):
                act.wait_ge(q_ps, h + 1)
                nc.scalar.activation(qT[:, h * GT:(h + 1) * GT], ps[:, 6 + h, :], ACT.Identity,
                                     bias=cols_s[:, 2:3]).then_inc(q_ready, 1)
            spread_out(qx, 0, 2)
            spread_out(qx, 0, 3)
            act.wait_ge(relb_ps, 1)
            for r in range(2):
                nc.scalar.activation(relb[:, r:XH:2], ps[:, 6 + r, r:XH:2], ACT.Copy).then_inc(relb_ready, 1)
            chunk_out(1)
            for i in range(CTX_SPLIT):
                ctx_out(i)
            att_out(0)
            chunk_out(2)
            for i in range(CTX_SPLIT, len(CTX_UNITS)):
                ctx_out(i)
            att_out(1)
            chunk_out(3)
            att_out(2)
            att_out(3)

            def queries_out(g):
                act.wait_ge(qnT_ps, g + 1)
                nc.scalar.activation(qT[:, g * GT:(g + 1) * GT], ps[:, 2 + g, :], ACT.Copy).then_inc(qT_ready, 1)

            def hq_out(g, p):
                act.wait_ge(hq_ps, g * PAIRS + p + 1)
                nc.scalar.activation(hqu[:, p, :], ps[:, hq_bank(g, p), :], ACT.Identity,
                                     scale=SCALE, bias=small[:, 1:2]).then_inc(hq_ev, 1)

            def z3_out(g):
                act.wait_ge(z3T_ps, g + 1)
                nc.scalar.activation(qT[:, g * GT:(g + 1) * GT], ps[:, 4, :], ACT.Copy).then_inc(z3T_ready, 1)

            def gate_act(g, i):
                u = g * HCH + i
                act.wait_ge(up_ps, u + 1)
                if u >= 4:
                    act.wait_ge(hid_ready, u - 3)
                nc.scalar.activation(gact[:, u % 4, :], ps[:, (u % 2) * 2, :], ACT.Silu).then_inc(act_ready, 1)

            queries_out(0)
            for p in range(PAIRS):
                hq_out(0, p)
            queries_out(1)
            for g in range(NG):
                if g:
                    for p in range(2 * HQ_EARLY, PAIRS):
                        hq_out(g, p)
                act.wait_ge(relb_ready, 2)
                for n in range(XH):
                    act.wait_ge(w_ps, g * XH + n + 1)
                    nc.scalar.activation(
                        wrel.rearrange("p i (b n) -> p b i n", n=XH)[:, :, :, n],
                        ps[:, n % 4, :].rearrange("p (b i) -> p b i", b=GB),
                        ACT.Identity, bias=relb[:, n:n + 1]).then_inc(w_ev, 1)
                if g:
                    z3_out(0)
                act.wait_ge(gate_ps, g + 1)
                nc.scalar.activation(gate[:, :, :],
                                     ps[:, 7, 128:128 + GB * XH].rearrange("p (b n) -> p b n", b=GB),
                                     ACT.Tanh, scale=0.5).then_inc(gate_t, 1)
                for i in range(STEPS):
                    k = g * NU + i
                    if i < NU:
                        b, q4 = k // 4, k % 4
                        act.wait_ge(max_ready, k + 1)
                        if k >= 4:
                            act.wait_ge(pT_ps, k - 3)
                        for h in range(4):
                            n = b * XH + head(q4, h)
                            ins = nc.scalar.activation(pbuf[:, k % 4, h, :], ps[:, i % 3, h * J:(h + 1) * J],
                                                       ACT.Exp, bias=nmax[:, 4 * k + h:4 * k + h + 1],
                                                       accum_out=rsum[:, n:n + 1])
                        ins.then_inc(p_ready, 1)
                    if g == 1 and i == 9:
                        act.wait_ge(route_sub, 1)
                        nc.scalar.activation(rt[:, 2, :, :], rt[:, 1, :, :], ACT.Exp).then_inc(route_exp, 1)
                    for h in range(2):
                        if (bl := due(i, OT_AT[h])) is not None:
                            b = g * GB + bl
                            act.wait_ge(oT_ps, 2 * b + h + 1)
                            nc.scalar.activation(oT[:, 4 * h:4 * h + 4, :],
                                                 ps[:, 7, :].rearrange("p (a i) -> p a i", a=4),
                                                 ACT.Copy).then_inc(oT_ready, 1)
                    if g == 0 and NU <= i < NU + HQ_EARLY:
                        hq_out(1, 2 * (i - NU))
                        hq_out(1, 2 * (i - NU) + 1)
                    if g == 1 and i >= UP_FROM:
                        gate_act(0, i - UP_FROM)

            for i in range(UP_EARLY, HCH):
                gate_act(0, i)
            z3_out(1)
            for i in range(HCH):
                gate_act(1, i)
                if i == 3:
                    act.wait_ge(route_sub, 2)
                    nc.scalar.activation(rt[:, 2, :, :], rt[:, 1, :, :], ACT.Exp).then_inc(route_exp, 1)

        @block.vector
        def _(dve):
            count = [0]
            norms = [0]

            def own(ins):
                ins.then_inc(vec, 1)
                count[0] += 1

            def settle():
                dve.wait_ge(vec, count[0])

            def stats(src, b0, b1):
                for b in range(b0, b1):
                    own(nc.vector.bn_stats(st[:, b, :], src[:, b, :]))

            def aggregate(b0, b1):
                settle()
                for b in range(b0, b1):
                    own(nc.vector.bn_aggr(mv[:, b, :], st[:, b, :]))

            def variance(b0, b1):
                settle()
                nc.vector.tensor_scalar(var[:, b0:b1], mv[:, b0:b1, 1], LN_EPS, None, ALU.add).then_inc(var_ready, 1)
                norms[0] += 1

            def normalise(dst, src, b0, b1, n, ready=None):
                dve.wait_ge(rs_ready, n)
                for b in range(b0, b1):
                    ins = nc.vector.tensor_scalar(dst[:, b, :], src[:, b, :], mv[:, b, 0:1], rs[:, b:b + 1],
                                                  ALU.subtract, ALU.mult)
                    if ready is None:
                        own(ins)
                    else:
                        ins.then_inc(ready, 1)

            own(nc.vector.memset(hist[:, :, :, :], 0.0))
            own(nc.vector.memset(terms[:, :, :, :], 0.0))
            settle()
            own(nc.vector.memset(hist[:, :, :, DH], 1.0))
            for h in range(2):
                dve.wait_ge(ld[f"x{h}"], 16)
                stats(xs, h * GB, (h + 1) * GB)
                aggregate(h * GB, (h + 1) * GB)
                variance(h * GB, (h + 1) * GB)
            dve.wait_ge(ld["cols"], 16)
            nc.vector.tensor_scalar(small[:, 0:1], cols_s[:, 5:6], 0.5, None, ALU.mult)
            own(nc.vector.tensor_scalar(small[:, 1:2], cols_s[:, 6:7], SCALE, None, ALU.mult))
            own(nc.vector.tensor_tensor(small[:, 2:3], cols_s[:, 7:8], cols_s[:, 6:7], ALU.subtract))
            for h in range(2):
                normalise(xn, xs, h * GB, (h + 1) * GB, h + 1, xn_ready)
                dve.wait_ge(xn_ready, (h + 1) * GB)
                stats(xn, h * GB, (h + 1) * GB)
                aggregate(h * GB, (h + 1) * GB)
                variance(h * GB, (h + 1) * GB)
            nc.vector.tensor_scalar(small[:, 3:4], small[:, 2:3], SCALE, None, ALU.mult).then_inc(small_ready, 1)
            for h in range(2):
                normalise(z, xn, h * GB, (h + 1) * GB, h + 3, z_ready)

            dve.wait_ge(norm_ready, 2)
            own(nc.vector.tensor_scalar(sq, sq, NORM_EPS, None, ALU.max))
            settle()
            own(nc.vector.reciprocal(sq, sq))
            dve.wait_ge(beta_ready, 2)
            own(nc.vector.tensor_scalar(beta, beta, 0.5, 0.5, ALU.mult, ALU.add))
            settle()
            own(nc.vector.tensor_tensor(beta, beta, sq, ALU.mult))
            settle()
            own(nc.vector.scalar_tensor_tensor(fT[:, :], beta, -1.0, sq, ALU.mult, ALU.mult))
            settle()
            fv = fT[:, :].rearrange("p (b t) -> p b t", b=B)
            gv = gT.rearrange("p (b t) -> p b t", b=B)
            dve.wait_ge(kk_ps, 2)
            own(nc.vector.memset(gv[:, :, T - 1:T], 0.0))
            for h in range(2):
                nc.vector.tensor_tensor(gv[:, h * GB:(h + 1) * GB, 0:T - 1],
                                        ps[:, 4 + h, :].rearrange("p (b t) -> p b t", b=GB)[:, :, 0:T - 1],
                                        fv[:, h * GB:(h + 1) * GB, 1:T], ALU.mult).then_inc(share_ready, 1)
            dve.wait_ge(v_ready, 2)
            settle()
            nc.vector.tensor_tensor(vT, vT, beta, ALU.mult).then_inc(values_ready, 1)

            def reads(c):
                dve.wait_ge(kx_ready, c + 1)
                ft = fT[:, :].rearrange("p (b t) -> p t b", b=B)[:, c * CH:(c + 1) * CH, :]
                own(nc.vector.tensor_tensor(mx[:, c % 2, :, :, 0:DH], kx[:, c % 2, :, :, 0:DH],
                                            ft.unsqueeze(3).to_broadcast([128, CH, B, DH]), ALU.mult))
                settle()

            def read_state(t, prev):
                return nc.vector.tensor_tensor(terms[:, (t - 1) % 2, :, DH + 1:], hist[:, prev % CH, :, :],
                                               mx[:, (t // CH) % 2, t % CH, :, :], ALU.mult)

            def update(t):
                return nc.vector.tensor_reduce(upd[:, t % 2, :], terms[:, (t - 1) % 2, :, DH:], AX, ALU.add)

            reads(0)
            own(read_state(0, -1))
            settle()
            update(0).then_inc(scan_step, 1)
            for t in range(T):
                c, s = t // CH, t % CH
                done = 1 + 4 * t
                if s == CH - 1 and t < T - 1:
                    reads(c + 1)
                dve.wait_ge(scan_step, done)
                nc.vector.tensor_tensor(terms[:, t % 2, :, 0:DH + 1], kx[:, c % 2, s, :, :],
                                        upd[:, t % 2, :].unsqueeze(2).to_broadcast([128, B, DH + 1]),
                                        ALU.mult).then_inc(scan_step, 1)
                if t < T - 1:
                    read_state(t + 1, t - 1).then_inc(scan_step, 1)
                dve.wait_ge(scan_step, done + 1)
                nc.vector.tensor_tensor(hist[:, t % CH, :, 0:DH], hist[:, (t - 1) % CH, :, 0:DH],
                                        terms[:, t % 2, :, 0:DH], ALU.add).then_inc(scan_step, 1)
                if t < T - 1:
                    dve.wait_ge(scan_step, done + 2)
                    update(t + 1).then_inc(scan_step, 1)
                if s == CH - 1:
                    dve.wait_ge(scan_step, done + (3 if t < T - 1 else 2))
                    dve.wait_ge(spread_ev, 4 * c + 4)
                    nc.vector.tensor_tensor(qx[:, c % 2, :, :, :], hist[:, :, :, 0:DH], qx[:, c % 2, :, :, :],
                                            ALU.mult).then_inc(scan_done, 1)

            dve.wait_ge(base_ready, 1)
            for g in range(NG):
                b0, b1 = g * GB, (g + 1) * GB
                dve.wait_ge(x2_ps, g + 1)
                own(nc.vector.tensor_tensor(xs[:, b0:b1, :], xs[:, b0:b1, :],
                                            ps[:, g, :].rearrange("p (b c) -> p b c", b=GB), ALU.add))
                settle()
                stats(xs, b0, b1)
                aggregate(b0, b1)
                variance(b0, b1)
            for g in range(NG):
                normalise(qn, xs, g * GB, (g + 1) * GB, 5 + g, qn_ready)

            def scale_half(b, h):
                bl, hs = b % GB, slice(8 * h, 8 * h + 8)
                own(nc.vector.reciprocal(rden[:, hs], rsum[:, b * XH + 8 * h:b * XH + 8 * h + 8]))
                settle()
                own(nc.vector.tensor_tensor(gate[:, bl, hs], gate[:, bl, hs], rden[:, hs], ALU.mult))
                settle()
                dve.wait_ge(o_ps, 4 * b + 2 * h + 2)
                if b >= 1:
                    dve.wait_ge(oT_ps, 2 * (b - 1) + h + 1)
                nc.vector.tensor_tensor(
                    osc[:, h * BANK:(h + 1) * BANK].rearrange("p (n d) -> p n d", d=DK),
                    ps[:, 5 + h, :].rearrange("p (n d) -> p n d", d=DK),
                    gate[:, bl, hs].unsqueeze(2).to_broadcast([128, 8, DK]), ALU.mult).then_inc(osc_ready, 1)

            def post(g, stage):
                b0, b1 = g * GB, (g + 1) * GB
                if stage == 0:
                    dve.wait_ge(y_ready, b1)
                    stats(qn, b0, b1)
                elif stage == 1:
                    aggregate(b0, b1)
                elif stage == 2:
                    variance(b0, b1)
                elif stage == 3:
                    normalise(qn, qn, b0, b1, 7 + 2 * g)
                elif stage == 4:
                    settle()
                    own(nc.vector.tensor_tensor(qn[:, b0:b1, :], qn[:, b0:b1, :],
                                                rows_s[:, 1:2, :].to_broadcast([128, GB, C]), ALU.mult))
                elif stage == 5:
                    settle()
                    own(nc.vector.tensor_tensor(qn[:, b0:b1, :], qn[:, b0:b1, :],
                                                rows_s[:, 2:3, :].to_broadcast([128, GB, C]), ALU.add))
                elif stage == 6:
                    settle()
                    own(nc.vector.tensor_tensor(xs[:, b0:b1, :], xs[:, b0:b1, :], qn[:, b0:b1, :], ALU.add))
                elif stage == 7:
                    settle()
                    stats(xs, b0, b1)
                elif stage == 8:
                    aggregate(b0, b1)
                elif stage == 9:
                    variance(b0, b1)
                else:
                    normalise(qn, xs, b0, b1, 8 + 2 * g, z3_ready)
            POST = 11

            def logits(g):
                dve.wait_ge(route_ps, g + 1)
                nc.vector.tensor_copy(rt[:, 0, :, :], ps[:, 4, 0:GB * EXP].rearrange("p (b e) -> p b e", b=GB)
                                      ).then_inc(logits_ready, 1)

            def route(g, stage):
                logit = rt[:, 0, :, :]
                top1 = rt[:, 3, :, 0:1].to_broadcast([128, GB, EXP])
                top2 = rt[:, 3, :, 1:2].to_broadcast([128, GB, EXP])
                settle()
                if stage == 0:
                    dve.wait_ge(logits_ready, g + 1)
                    for b in range(GB):
                        own(nc.vector.max(rt[:, 3, b, :], rt[:, 0, b, :]))
                elif stage == 1:
                    nc.vector.tensor_tensor(rt[:, 1, :, :], logit, top1, ALU.subtract).then_inc(route_sub, 1)
                    own(nc.vector.tensor_tensor(rt[:, 4, :, :], logit, top2, ALU.is_gt))
                    own(nc.vector.tensor_tensor(rt[:, 5, :, :], logit, top2, ALU.is_equal))
                elif stage == 2:
                    own(nc.vector.tensor_reduce(rt[:, 8, :, 0], rt[:, 4, :, :], AX, ALU.add))
                    own(nc.vector.tensor_copy(rt[:, 6, :, :], rt[:, 5, :, :]))
                elif stage in (3, 4, 5):
                    d = 1 << (stage - 3)
                    a, b_ = (6, 7) if stage != 4 else (7, 6)
                    own(nc.vector.tensor_copy(rt[:, b_, :, 0:d], rt[:, a, :, 0:d]))
                    own(nc.vector.tensor_tensor(rt[:, b_, :, d:EXP], rt[:, a, :, d:EXP],
                                                rt[:, a, :, 0:EXP - d], ALU.add))
                elif stage == 6:
                    own(nc.vector.tensor_tensor(rt[:, 6, :, :], rt[:, 7, :, :],
                                                rt[:, 8, :, 0:1].to_broadcast([128, GB, EXP]), ALU.add))
                elif stage == 7:
                    own(nc.vector.scalar_tensor_tensor(rt[:, 7, :, :], rt[:, 6, :, :], 2.0, rt[:, 5, :, :],
                                                       ALU.is_le, ALU.mult))
                elif stage == 8:
                    own(nc.vector.tensor_tensor(rt[:, 4, :, :], rt[:, 4, :, :], rt[:, 7, :, :], ALU.add))
                elif stage == 9:
                    dve.wait_ge(route_exp, g + 1)
                    own(nc.vector.tensor_tensor(rt[:, 9, :, :], rt[:, 2, :, :], rt[:, 4, :, :], ALU.mult))
                elif stage == 10:
                    own(nc.vector.tensor_reduce(rt[:, 10, :, 0], rt[:, 9, :, :], AX, ALU.add))
                elif stage == 11:
                    own(nc.vector.reciprocal(rt[:, 11, :, 0], rt[:, 10, :, 0]))
                elif stage == 12:
                    own(nc.vector.tensor_tensor(pw[:, g * GB:(g + 1) * GB, :], rt[:, 9, :, :],
                                                rt[:, 11, :, 0:1].to_broadcast([128, GB, EXP]), ALU.mult))
            ROUTE = 13

            def hidden(g, i):
                u = g * HCH + i
                dve.wait_ge(act_ready, u + 1)
                if i == 0 and g:
                    dve.wait_ge(down_ps, g * GB * 3)
                nc.vector.tensor_tensor(hid[:, i, :], gact[:, u % 4, :], ps[:, (u % 2) * 2 + 1, :],
                                        ALU.mult).then_inc(hid_ready, 1)

            def experts_sum(b):
                for m in range(3):
                    u = b * 3 + m
                    bank = 4 + u % 3
                    dve.wait_ge(down_ps, u + 1)
                    if m == 0:
                        nc.vector.tensor_tensor(y3[:, b, :], ps[:, bank, 0:C], xs[:, b, :],
                                                ALU.add).then_inc(down_used, 1)
                        continue
                    if m == 1:
                        dve.wait_ge(down_used, u)
                    for e in range(4):
                        ex = expert(m, e)
                        if e or m == 2:
                            settle()
                            dve.wait_ge(down_used, u)
                        ins = nc.vector.scalar_tensor_tensor(
                            y3[:, b, :], ps[:, bank, e * C:(e + 1) * C], pw[:, b, ex:ex + 1],
                            y3[:, b, :], ALU.mult, ALU.add)
                        if e == 3:
                            ins.then_inc(down_used, 1)
                        else:
                            own(ins)

            for g in range(NG):
                if g:
                    for stage in range(POST):
                        post(0, stage)
                dve.wait_ge(mask_ready, 1)
                for i8 in range(T // 8):
                    u = g * (T // 8) + i8
                    dve.wait_ge(rel_ps, u + 1)
                    nc.vector.tensor_tensor(
                        relT[:, :, 8 * i8:8 * i8 + 8].rearrange("p (b n) i -> p i b n", b=GB),
                        ps[0:J, i8 % 4, :].rearrange("p (i b n) -> p i b n", i=8, b=GB),
                        maskadd[:, g * GB:(g + 1) * GB, 8 * i8:8 * i8 + 8]
                        .rearrange("p b i -> p i b").unsqueeze(3).to_broadcast([J, 8, GB, XH]),
                        ALU.add).then_inc(rel_ev, 1)
                if g:
                    logits(0)
                dve.wait_ge(gate_t, g + 1)
                own(nc.vector.tensor_scalar(gate[:, :, :], gate[:, :, :], 0.5, 0.5, ALU.mult, ALU.add))
                settle()
                for i in range(STEPS):
                    k = g * NU + i
                    if i < NU:
                        dve.wait_ge(s_ps, k + 1)
                        nc.vector.tensor_reduce(nmax[:, 4 * k:4 * k + 4],
                                                ps[:, i % 3, 0:4 * J].rearrange("p (h j) -> p h j", h=4),
                                                AX, ALU.max, negate=True).then_inc(max_ready, 1)
                    if TURN <= i < NU + TURN:
                        kt = k - TURN
                        dve.wait_ge(pT_ps, kt + 1)
                        if kt >= 4:
                            dve.wait_ge(o_ps, kt - 3)
                        nc.vector.tensor_copy(pT[:, kt % 4, :, :],
                                              ps[0:J, 3 + kt % 2, :].rearrange("p (h i) -> p h i", h=4)
                                              ).then_inc(pT_ready, 1)
                    for h in range(2):
                        if (bl := due(i, SCALE_AT[h])) is not None:
                            scale_half(g * GB + bl, h)
                    if (bl := due(i, SUM_AT)) is not None:
                        b = g * GB + bl
                        dve.wait_ge(y_ps, b + 1)
                        nc.vector.tensor_tensor(qn[:, b, :], qn[:, b, :], ps[:, 7, 0:C], ALU.add).then_inc(y_ready, 1)
                    if g and 2 <= i < 2 + ROUTE:
                        route(0, i - 2)
                    if g and i >= UP_FROM:
                        hidden(0, i - UP_FROM)

            for i in range(UP_EARLY, HCH):
                hidden(0, i)
                for stage in (2 * (i - UP_EARLY), 2 * (i - UP_EARLY) + 1):
                    if stage < POST:
                        post(1, stage)
            logits(1)
            for b in range(GB):
                experts_sum(b)
            for i in range(HCH):
                hidden(1, i)
                if i < ROUTE:
                    route(1, i)
            for b in range(GB, B):
                experts_sum(b)

        @block.tensor
        def _(pe):
            pe.wait_ge(ld["ident"], 16)
            for b in range(B):
                pe.wait_ge(z_ready, b + 1)
                ins = nc.tensor.transpose(ps[:, b // GB, (b % GB) * T:(b % GB + 1) * T], z[:, b, :], ident[:, :])
                if b % GB == GB - 1:
                    ins.then_inc(zT_ps, 1)
            pe.wait_ge(ld["wqkvb"], 16)

            def project(m, bank, done):
                for h in range(2):
                    pe.wait_ge(nT_ready, h + 1)
                    nc.tensor.matmul(ps[:, bank + h, :], wqkvb_s[:, m * C:(m + 1) * C], nT[:, h * GT:(h + 1) * GT],
                                     start=True, stop=True).then_inc(done, 1)

            def spread(c, u):
                src = kT if u < 2 else qT[:, :]
                for j in range(4):
                    ins = nc.tensor.matmul(
                        ps[:, 2 * (u % 2) + j // 2, (j % 2) * 256:(j % 2) * 256 + 256],
                        sel[:, 4 * (u % 2) + j, :],
                        src.rearrange("p (b t) -> p b t", b=B)[:, :, c * CH:(c + 1) * CH],
                        start=True, stop=True)
                ins.then_inc(spread_ps, 1)

            def spread_chunk(c):
                for u in range(4):
                    pe.wait_ge(spread_ev, 4 * c + u - 1)
                    spread(c, u)

            def head_sums(src, ready, bank, done):
                for h in range(2):
                    pe.wait_ge(ready, h + 1)
                    nc.tensor.matmul(ps[:, bank + h, :], same_head[:, :], src[:, h * GT:(h + 1) * GT],
                                     start=True, stop=True).then_inc(done, 1)

            project(1, 2, k_ps)
            pe.wait_ge(ld["same"], 16)
            head_sums(sq, sq_ready, 4, norm_ps)
            project(3, 6, beta_ps)
            pe.wait_ge(ld["sel"], 16)
            pe.wait_ge(kT_ready, 2)
            spread(0, 0)
            spread(0, 1)
            pe.wait_ge(norm_ready, 2)
            pe.wait_ge(kk_ready, 2)
            head_sums(kk, kk_ready, 4, kk_ps)
            pe.wait_ge(spread_ev, 1)
            project(2, 0, v_ps)
            pe.wait_ge(beta_ready, 2)
            project(0, 6, q_ps)
            pe.wait_ge(v_ready, 2)
            pe.wait_ge(q_ready, 2)
            spread(0, 2)
            pe.wait_ge(spread_ev, 2)
            spread(0, 3)

            def ctx_project(i):
                kind, a, h = CTX_UNITS[i]
                if i >= 3:
                    pe.wait_ge(ctxp_ev, i - 2)
                if kind == "k":
                    nc.tensor.matmul(ps[:, 4 + i % 3, 0:GB * J], Wk_s[:, h * 128:(h + 1) * 128],
                                     ctxT_s[:, a * GB:(a + 1) * GB, :],
                                     start=True, stop=True).then_inc(ctxp_ps, 1)
                else:
                    nc.tensor.matmul(ps[0:J, 4 + i % 3, :], ctxT_s[:, a, :], Wv_s[:, h * BANK:(h + 1) * BANK],
                                     start=True, stop=True).then_inc(ctxp_ps, 1)

            def attend(c):
                pe.wait_ge(scan_done, c + 1)
                if c >= 1:
                    pe.wait_ge(att_ev, c)
                for j in range(DH):
                    ins = nc.tensor.matmul(ps[:, 7, (c % 2) * 256:(c % 2) * 256 + 256], wout_s,
                                           qx[:, c % 2, :, :, j].rearrange("p t b -> p b t"),
                                           start=(j == 0), stop=(j == DH - 1))
                ins.then_inc(att_ps, 1)

            pe.wait_ge(ld["Wr"], 16)
            pe.wait_ge(small_ready, 1)
            for n in range(XH):
                r = 64 * (n % 2)
                ins = nc.tensor.matmul(ps[:, 6 + n % 2, n:n + 1], WrT_s[r:r + 64, n // 2, :], small[r:r + 64, 3:4],
                                       start=True, stop=True)
            ins.then_inc(relb_ps, 1)
            spread_chunk(1)
            pe.wait_ge(ld["ctx"], 16)
            pe.wait_ge(ld["Wk"], 16)
            pe.wait_ge(ld["Wv"], 16)
            pe.wait_ge(ld["wout"], 16)
            pe.wait_ge(relb_ready, 2)
            pe.wait_ge(share_ready, 2)
            for i in range(CTX_SPLIT):
                ctx_project(i)
            attend(0)
            spread_chunk(2)
            for i in range(CTX_SPLIT, len(CTX_UNITS)):
                ctx_project(i)
            attend(1)
            spread_chunk(3)
            attend(2)
            attend(3)
            pe.wait_ge(att_ev, 4)
            pe.wait_ge(spread_ev, 4 * NC)
            for b in range(B):
                ins = nc.tensor.transpose(ps[:, b // GB, (b % GB) * C:(b % GB + 1) * C],
                                          attT[:, b * T:(b + 1) * T], ident[:, :])
                if b % GB == GB - 1:
                    ins.then_inc(x2_ps, 1)

            def queries(g):
                for bl in range(GB):
                    pe.wait_ge(qn_ready, g * GB + bl + 1)
                    ins = nc.tensor.transpose(ps[:, 2 + g, bl * T:(bl + 1) * T], qn[:, g * GB + bl, :], ident[:, :])
                ins.then_inc(qnT_ps, 1)

            def hq_project(g, p):
                back = 4 if g == 0 else 3
                if p >= back:
                    pe.wait_ge(hq_ev, g * PAIRS + p - back + 1)
                nc.tensor.matmul(ps[:, hq_bank(g, p), :], Wq_s[:, p * 128:(p + 1) * 128],
                                 qT[:, g * GT:(g + 1) * GT], start=True, stop=True).then_inc(hq_ps, 1)

            def scores(g, i):
                k = g * NU + i
                b, q4 = k // 4, k % 4
                bl = b % GB
                if i >= 3:
                    pe.wait_ge(p_ready, k - 2)
                for h in range(4):
                    n = head(q4, h)
                    r = 64 * (n % 2)
                    nc.tensor.matmul(ps[:, i % 3, h * J:(h + 1) * J], relT[:, bl * XH + n, :],
                                     ident[0:J, 0:J], is_transpose=True, start=True, stop=False)
                    ins = nc.tensor.matmul(ps[:, i % 3, h * J:(h + 1) * J],
                                           hqu[r:r + 64, n // 2, bl * T:(bl + 1) * T],
                                           hk[r:r + 64, n // 2, b, :], start=False, stop=True)
                ins.then_inc(s_ps, 1)

            def turn(k):
                pe.wait_ge(p_ready, k + 1)
                if k >= 2:
                    pe.wait_ge(pT_ready, k - 1)
                for h in range(4):
                    ins = nc.tensor.transpose(ps[0:J, 3 + k % 2, h * T:(h + 1) * T], pbuf[:, k % 4, h, :],
                                              ident[:, :])
                ins.then_inc(pT_ps, 1)

            def values(k):
                b, q4 = k // 4, k % 4
                pe.wait_ge(pT_ready, k + 1)
                if b >= 1 and q4 % 2 == 0:
                    pe.wait_ge(osc_ready, 2 * (b - 1) + q4 // 2 + 1)
                for h in range(4):
                    n = head(q4, h)
                    ins = nc.tensor.matmul(ps[:, 5 + n // 8, (n % 8) * DK:(n % 8 + 1) * DK],
                                           pT[:, k % 4, h, :], hv[:, b, n * DK:(n + 1) * DK],
                                           start=True, stop=True)
                ins.then_inc(o_ps, 1)

            def turn_outputs(b, h):
                pe.wait_ge(osc_ready, 2 * b + h + 1)
                if h:
                    pe.wait_ge(oT_ready, 2 * b + h)
                elif b:
                    pe.wait_ge(y_ready, b)
                if b % GB == 0:
                    pe.wait_ge(gate_t, b // GB + 1)
                for p in range(4):
                    ins = nc.tensor.transpose(ps[:, 7, p * T:(p + 1) * T],
                                              osc[:, (4 * h + p) * 128:(4 * h + p + 1) * 128], ident[:, :])
                ins.then_inc(oT_ps, 1)

            def last_product(b):
                pe.wait_ge(oT_ready, 2 * b + 2)
                for p in range(PAIRS):
                    ins = nc.tensor.matmul(ps[:, 7, 0:C], oT[:, p, :], Wo_s[:, p, :],
                                           start=(p == 0), stop=(p == PAIRS - 1))
                ins.then_inc(y_ps, 1)

            def turn_z3(g):
                for bl in range(GB):
                    pe.wait_ge(z3_ready, g * GB + bl + 1)
                    ins = nc.tensor.transpose(ps[:, 4, bl * T:(bl + 1) * T], qn[:, g * GB + bl, :], ident[:, :])
                ins.then_inc(z3T_ps, 1)

            def route(g):
                pe.wait_ge(z3T_ready, g + 1)
                for bl in range(GB):
                    b = g * GB + bl
                    ins = nc.tensor.matmul(ps[:, 4, bl * EXP:(bl + 1) * EXP], qT[:, b * T:(b + 1) * T], Wg_s[:, :],
                                           start=True, stop=True)
                ins.then_inc(route_ps, 1)

            def up(g, i):
                u = g * HCH + i
                if u >= 2:
                    pe.wait_ge(hid_ready, u - 1)
                nc.tensor.matmul(ps[:, (u % 2) * 2, :], W1_s[:, i, :], qT[:, g * GT:(g + 1) * GT],
                                 start=True, stop=True)
                nc.tensor.matmul(ps[:, (u % 2) * 2 + 1, :], W2_s[:, i, :], qT[:, g * GT:(g + 1) * GT],
                                 start=True, stop=True).then_inc(up_ps, 1)

            def down(g):
                pe.wait_ge(hid_ready, (g + 1) * HCH)
                for bl in range(GB):
                    b = g * GB + bl
                    tok = slice(bl * T, (bl + 1) * T)
                    for m in range(3):
                        u = b * 3 + m
                        bank = 4 + u % 3
                        if u >= 3:
                            pe.wait_ge(down_used, u - 2)
                        if m == 0:
                            for s in range(3):
                                r = 128 if s < 2 else SHID - 256
                                ins = nc.tensor.matmul(ps[:, bank, 0:C], hid[0:r, 12 + s, tok],
                                                       W3_s[0:r, 12 + s, :], start=(s == 0), stop=(s == 2))
                        else:
                            for e in range(4):
                                ex = expert(m, e)
                                r = 64 * (ex % 2)
                                nc.tensor.matmul(ps[:, bank, e * C:(e + 1) * C], hid[:, ex, tok],
                                                 W3_s[:, ex, :], start=True, stop=False)
                                ins = nc.tensor.matmul(ps[:, bank, e * C:(e + 1) * C],
                                                       hid[r:r + REST, EXP + ex // 2, tok],
                                                       W3_s[r:r + REST, EXP + ex // 2, :],
                                                       start=False, stop=True)
                        ins.then_inc(down_ps, 1)

            queries(0)
            pe.wait_ge(ld["Wq"], 16)
            pe.wait_ge(ld["Wo"], 16)
            pe.wait_ge(ld["tail"], 48)
            pe.wait_ge(qT_ready, 1)
            for p in range(PAIRS):
                hq_project(0, p)
            queries(1)
            pe.wait_ge(qT_ready, 2)
            for g in range(NG):
                if g:
                    for p in range(2 * HQ_EARLY, PAIRS):
                        hq_project(g, p)
                    pe.wait_ge(pT_ready, g * NU)
                pe.wait_ge(hq_ev, (g + 1) * PAIRS)
                for n in range(XH):
                    r = 64 * (n % 2)
                    if n >= 4:
                        pe.wait_ge(w_ev, g * XH + n - 3)
                    nc.tensor.matmul(ps[:, n % 4, :], WrT_s[r:r + 64, n // 2, :], hqu[r:r + 64, n // 2, :],
                                     start=True, stop=True).then_inc(w_ps, 1)
                if g:
                    turn_z3(0)
                pe.wait_ge(w_ev, (g + 1) * XH)
                for i in range(T):
                    if i % 8 == 0 and i >= 32:
                        pe.wait_ge(rel_ev, g * (T // 8) + i // 8 - 3)
                    ins = nc.tensor.matmul(ps[0:J, (i // 8) % 4, (i % 8) * 64:(i % 8 + 1) * 64],
                                           rel_s[:, T - 1 - i:T - 1 - i + J], wrel[:, i, :],
                                           start=True, stop=True)
                    if i % 8 == 7:
                        ins.then_inc(rel_ps, 1)
                if g:
                    route(0)
                    pe.wait_ge(y_ready, g * GB)
                for bl in range(GB):
                    b = g * GB + bl
                    ins = nc.tensor.matmul(ps[:, 7, 128 + bl * XH:128 + (bl + 1) * XH],
                                           qT[:, b * T:(b + 1) * T], hw_s[:, :], start=True, stop=True)
                ins.then_inc(gate_ps, 1)
                pe.wait_ge(rel_ev, (g + 1) * (T // 8))
                if g:
                    pe.wait_ge(logits_ready, 1)
                for i in range(STEPS):
                    k = g * NU + i
                    if i < NU:
                        scores(g, i)
                    if TURN <= i < NU + TURN:
                        turn(k - TURN)
                    if VALUES <= i < NU + VALUES:
                        values(k - VALUES)
                    for h in range(2):
                        if (bl := due(i, OT_AT[h])) is not None:
                            turn_outputs(g * GB + bl, h)
                    if (bl := due(i, Y_AT)) is not None:
                        last_product(g * GB + bl)
                    if g == 0 and NU <= i < NU + HQ_EARLY:
                        if i == NU:
                            pe.wait_ge(p_ready, NU)
                        hq_project(1, 2 * (i - NU))
                        hq_project(1, 2 * (i - NU) + 1)
                    if g == 1 and i >= UP_FROM:
                        if i == UP_FROM:
                            pe.wait_ge(ld["moe"], 48)
                            pe.wait_ge(p_ready, NG * NU)
                            pe.wait_ge(pT_ready, NG * NU)
                        up(0, i - UP_FROM)

            for i in range(UP_EARLY, HCH):
                up(0, i)
            turn_z3(1)
            route(1)
            pe.wait_ge(logits_ready, 2)
            down(0)
            for i in range(HCH):
                up(1, i)
            down(1)


def _layout(i):
    import numpy as np
    a = {k: np.asarray(v) for k, v in i.items()}

    def heads(w):
        return np.ascontiguousarray(w.reshape(C, DK, XH).transpose(0, 2, 1).reshape(C, XH * DK))

    def by_pair(w):
        return np.ascontiguousarray(w.reshape(DK, PAIRS, 2, C).transpose(2, 0, 1, 3).reshape(128, PAIRS, C))

    freq = (1.0 / 10000.0 ** (np.arange(0, C, 2, dtype=np.float32) / np.float32(C))).astype(np.float32)
    pos = np.arange(T - 1, -J, -1).astype(np.float32)
    ang = pos[:, None] * freq[None, :]
    emb = np.stack([np.sin(ang) * np.float32(0.1 * C), np.cos(ang) * np.float32(0.1 * C)], -1)
    rel = np.ascontiguousarray(emb.reshape(NREL, C).T.astype(np.float32))

    p = np.arange(128)
    ident = (p[:, None] == p[None, :]).astype(np.float32)
    same = (p[:, None] // DH == p[None, :] // DH).astype(np.float32)
    sel = np.stack([same * (p[:, None] % DH == j) for j in range(DH)], 1).astype(np.float32)
    consts = np.concatenate([ident, same, sel.reshape(128, DH * 128)], 1)

    def up(w, ws):
        o = np.zeros((C, HCH, 128), np.float32)
        o[:, :EXP] = w[:, :, :128].transpose(1, 0, 2)
        for e in range(EXP):
            r = 64 * (e % 2)
            o[:, EXP + e // 2, r:r + REST] = w[e, :, 128:]
        o[:, 12] = ws[:, 0:128]
        o[:, 13] = ws[:, 128:256]
        o[:, 14, :SHID - 256] = ws[:, 256:]
        return o

    w3 = np.zeros((128, HCH, C), np.float32)
    w3[:, :EXP] = a["L0_ffn_W3"][:, :128].transpose(1, 0, 2)
    for e in range(EXP):
        r = 64 * (e % 2)
        w3[r:r + REST, EXP + e // 2] = a["L0_ffn_W3"][e, 128:]
    w3[:, 12] = a["L0_ffn_Ws3"][0:128]
    w3[:, 13] = a["L0_ffn_Ws3"][128:256]
    w3[:SHID - 256, 14] = a["L0_ffn_Ws3"][256:]

    bq = a["L0_attn_b_qkvb"].reshape(4, C)
    twice = lambda v: np.concatenate([v, v])
    cols = np.stack([a["L0_attn_ln_g"], a["L0_attn_ln_b"], bq[0], bq[1], bq[2], bq[3],
                     twice(a["L0_xattn_ub_w"]), twice(a["L0_xattn_vb_w"])], 1)
    rows = np.stack([a["L0_attn_b_out"], a["L0_xattn_ln_g"], a["L0_xattn_ln_b"]])
    return {
        "x": a["x"],
        "ctxT": np.ascontiguousarray(a["ctx_1024"].transpose(2, 0, 1)),
        "maskT": np.ascontiguousarray(a["mask_BxSxS2_bf0"].transpose(2, 0, 1)),
        "w_qkvb": a["L0_attn_w_qkvb"], "w_out": a["L0_attn_w_out"], "cols": cols, "rows": rows,
        "consts": consts,
        "Wq": heads(a["L0_xattn_Wq"]), "Wk": heads(a["L0_xattn_Wk"]), "Wv": heads(a["L0_xattn_Wv"]),
        "WrT": by_pair(np.ascontiguousarray(a["L0_xattn_Wr"].T)),
        "Wo": by_pair(a["L0_xattn_Wo"]), "head_w": a["L0_xattn_head_w"], "rel_tab": rel,
        "Wg": a["L0_ffn_Wg"], "W1": up(a["L0_ffn_W1"], a["L0_ffn_Ws1"]),
        "W2": up(a["L0_ffn_W2"], a["L0_ffn_Ws2"]), "W3": w3,
    }


def kernel(**inputs):
    import numpy as np
    import concourse.bacc as bacc
    from concourse import mybir as mb
    from concourse.bass_utils import run_bass_kernel_spmd

    laid = _layout(inputs)
    nc = bacc.Bacc("TRN2", target_bir_lowering=False, num_devices=1)
    arrays, args = {}, []
    for name, a in laid.items():
        a = np.ascontiguousarray(a)
        arrays[f"in_{name}"] = a
        args.append(nc.dram_tensor(f"in_{name}", a.shape, mb.dt.from_np(a.dtype), kind="ExternalInput").ap())
    args.append(nc.dram_tensor("out", (B, T, C), mb.dt.float32, kind="ExternalOutput").ap())
    layer(nc, *args)
    r = run_bass_kernel_spmd(nc, [arrays], core_ids=[0])
    return r.results[0]["out"]
```

```python
import concourse.bass as bass
from concourse import mybir
from contextlib import ExitStack

B, T, C = 8, 128, 128
NH, DH = 16, 8
CH = 16
NC = T // CH
J = 120
XH, DK = 16, 64
PAIRS = XH // 2
GB = 4
NG = B // GB
GT = GB * T
EXP, HID = 8, 176
REST = HID - 128
SHID = 352
HCH = EXP + EXP // 2 + 3
BANK = 512
LN_EPS = 1e-5
NORM_EPS = 1e-6
SCALE = float(C) ** -0.5
NEG = -2.0 ** 60


def layer(nc, x, ctxT, mask, w_qkvb, w_out, cols, rows, consts, Wq, Wk, WvT, WrT, Wo, head_w, rot_tab,
          Wg, W1, W2, W3, out):
    fp32 = mybir.dt.float32
    u8 = mybir.dt.uint8
    bf16 = mybir.dt.bfloat16
    ALU = mybir.AluOpType
    ACT = mybir.ActivationFunctionType
    AX = mybir.AxisListType.X

    ctx = ExitStack()
    with ctx:
        def sb(name, shape, dt=fp32):
            return ctx.enter_context(nc.sbuf_tensor(name, shape, dt))

        def sem(name):
            return ctx.enter_context(nc.semaphore(name))

        hk = sb("hk", [128, NG, PAIRS, GB, J])
        hvo = sb("hvo", [J, B, 4, 4 * C])
        xs = sb("xs", [128, B, C])
        qn = sb("qn", [128, B, C])
        qT = sb("qT", [128, B * T])
        Wq_s = sb("Wq_s", [128, XH * DK])
        WrT_s = sb("WrT_s", [128, PAIRS, C])
        Wo_s = qn
        turn_s = sb("turn_s", [128, 2 * T + J])
        ident = sb("ident", [128, 128])
        same_head = sb("same_head", [128, 128])
        hw_s = sb("hw_s", [128, XH])
        Wg_s = sb("Wg_s", [128, EXP])
        rows_s = sb("rows_s", [128, 3, C])
        cols_s = sb("cols_s", [128, 8])
        maskadd = sb("maskadd", [128, B, J], bf16)
        mask_s = sb("mask_s", [128, B, J], u8)
        ident_b = sb("ident_b", [128, 128], bf16)
        small = sb("small", [128, 16])
        relb = sb("relb", [128, XH])
        st = sb("st", [128, B, 6])
        mv = sb("mv", [128, B, 2])
        rs = sb("rs", [128, B])
        var = sb("var", [128, B])
        neg_half = sb("neg_half", [128, B])
        inv = sb("inv", [128, B * NH])
        nmax = sb("nmax", [128, XH * B])
        rsum = sb("rsum", [128, XH * B])
        gate = sb("gate", [128, B, XH])
        rden = sb("rden", [128, 2, GB])
        rt = sb("rt", [128, 12, GB, EXP])
        pw = sb("pw", [128, B, EXP])

        REGION = 19200
        region = sb("region", [128, REGION])
        at = [0]

        def cut(*shape, p=128):
            n = 1
            for s in shape:
                n *= s
            assert at[0] + n <= REGION, at[0] + n
            a = region[0:p, at[0]:at[0] + n]
            at[0] += n
            names = "abcd"[:len(shape)]
            if len(shape) == 1:
                return a
            return a.rearrange(f"p ({' '.join(names)}) -> p {' '.join(names)}",
                               **dict(zip(names, shape)))

        nT = cut(B * T)
        beta = cut(B * T)
        kx = cut(2, CH, B, DH + 1)
        mx = cut(2, CH, B, DH + 1)
        qx = cut(2, CH, B, DH)
        hist = cut(CH, B, DH + 1)
        xn = cut(B, C)
        z = cut(B, C)
        kT = cut(B * T)
        vT = cut(B * T)
        sel = cut(DH, 128)
        wqkvb_s = cut(4 * C)
        wout_s = cut(C)
        Wk_s = cut(XH * DK)
        WvT_s = cut(PAIRS, C)
        ctxT_s = cut(B, J)
        sq = z.rearrange("p b t -> p (b t)")
        VO = region[:, 0:XH * C].rearrange("p (q n) -> p q n", q=4)
        inv_x = vT
        attT = sq
        kk = xn.rearrange("p b t -> p (b t)")
        gT = kk
        at[0] = 0
        hqu = cut(4, GT)
        wsw = cut(2, GT)
        wrot = cut(4, GT)
        pbuf = cut(4, GB, J)
        pT = cut(4, GB, T, p=J)
        W1_s = cut(HCH, 128)
        W2_s = cut(HCH, 128)
        hid_head = cut(HCH - 3, GT)
        keys_used = hk[:, 0, :, :, :].rearrange("p a b j -> p (a b j)")
        W3_s = keys_used[:, 0:HCH * C].rearrange("p (i c) -> p i c", i=HCH)
        gact = keys_used[:, HCH * C:HCH * C + 3 * GT].rearrange("p (i n) -> p i n", i=3)

        def hid(i):
            return hid_head[:, i, :] if i < HCH - 3 else hqu[:, i - (HCH - 3), :]

        fT = sb("fT", [128, B * T])
        terms = sb("terms", [128, 2, B, 2 * DH + 2])
        upd = sb("upd", [128, 2, B])

        ps = ctx.enter_context(nc.psum_tensor("ps", [128, 8, BANK], fp32))

        ld = {n: sem("ld_" + n) for n in
              ["x0", "x1", "cols", "rows", "ident", "same", "sel", "wqkvb", "wout", "ctx", "Wk", "Wv", "Wq",
               "Wr", "Wo", "tail", "mask", "moe"]}
        var_ready = sem("var_ready")
        rs_ready = sem("rs_ready")
        xn_ready = sem("xn_ready")
        z_ready = sem("z_ready")
        zT_ps = sem("zT_ps")
        nT_ready = sem("nT_ready")
        k_ps = sem("k_ps")
        kT_ready = sem("kT_ready")
        sq_ready = sem("sq_ready")
        zero_ready = sem("zero_ready")
        table_ready = sem("table_ready")
        norm_ps = sem("norm_ps")
        norm_ready = sem("norm_ready")
        inv_spread = sem("inv_spread")
        inv_ps = sem("inv_ps")
        inv_used = sem("inv_used")
        small_ready = sem("small_ready")
        beta_ps = sem("beta_ps")
        beta_ready = sem("beta_ready")
        v_ps = sem("v_ps")
        v_ready = sem("v_ready")
        q_ps = sem("q_ps")
        q_ready = sem("q_ready")
        kk_ready = sem("kk_ready")
        kk_ps = sem("kk_ps")
        share_ready = sem("share_ready")
        values_ready = sem("values_ready")
        first_values = sem("first_values")
        spread_ps = sem("spread_ps")
        spread_ev = sem("spread_ev")
        kx_ready = sem("kx_ready")
        scan_step = sem("scan_step")
        scan_done = sem("scan_done")
        att_ps = sem("att_ps")
        att_ev = sem("att_ev")
        ctxp_ps = sem("ctxp_ps")
        ctxp_ev = sem("ctxp_ev")
        base_ready = sem("base_ready")
        mask_ready = sem("mask_ready")
        relb_ps = sem("relb_ps")
        relb_ready = sem("relb_ready")
        x2_ps = sem("x2_ps")
        qn_ready = sem("qn_ready")
        qnT_ps = sem("qnT_ps")
        qT_ready = sem("qT_ready")
        hq_ps = sem("hq_ps")
        hq_ev = sem("hq_ev")
        w_ps = sem("w_ps")
        w_swapped = sem("w_swapped")
        w_sines = sem("w_sines")
        w_cosines = sem("w_cosines")
        w_ready = sem("w_ready")
        s_ps = sem("s_ps")
        max_ready = sem("max_ready")
        p_ready = sem("p_ready")
        pT_ps = sem("pT_ps")
        pT_ready = sem("pT_ready")
        gate_ps = sem("gate_ps")
        gate_t = sem("gate_t")
        identb_ready = sem("identb_ready")
        p_scaled = sem("p_scaled")
        y_ps = sem("y_ps")
        y_ready = sem("y_ready")
        z3_ready = sem("z3_ready")
        z3T_ps = sem("z3T_ps")
        z3T_ready = sem("z3T_ready")
        route_ps = sem("route_ps")
        logits_ready = sem("logits_ready")
        route_sub = sem("route_sub")
        route_exp = sem("route_exp")
        up_ps = sem("up_ps")
        act_ready = sem("act_ready")
        hid_ready = sem("hid_ready")
        down_ps = sem("down_ps")
        down_used = sem("down_used")
        stored = sem("stored")
        vec = sem("vec")
        pool_own = sem("pool_own")

        CTX_UNITS = [("k", g, p) for g in range(NG) for p in range(PAIRS)] + \
                    [("vo", 0, q) for q in range(4)] + \
                    [("v", b, q) for b in range(B) for q in range(4)]
        CTX_PARTS = (6, 12, 18, 25, 27, 34, 40, 40, 44, 47, len(CTX_UNITS))
        SCAN_OPS = 5
        REL_BIAS_AT = 2
        CTX_LATE = T - 15
        TAIL = 8
        NU = NG * XH
        NP = NU // 2
        TURNED, SCORES, SCALED, TURN, VALUES = 1, 2, 3, 4, 5
        STEPS = NU + VALUES
        GATES_AT = (1, XH // 2)
        HALF = XH - 1 + VALUES
        POST_AT = {HALF + 1: (0, 1), HALF + 2: (2,), HALF + 3: (3, 4), HALF + 4: (5, 6), HALF + 5: (7, 8),
                   HALF + 6: (9,), HALF + 7: (10,)}
        Z3_AT = HALF + 8
        ROUTE_AT = Z3_AT + 1
        UP_FROM = NU + SCORES - 1
        UP_EARLY = STEPS - UP_FROM
        DOWN = (1, 2, 0)
        ROUTE_BESIDE = ((), (0, 1), (2, 3, 4, 5, 6, 7, 8), (9, 10, 11, 12))
        S_BANK, W_BANKS, HQ_BANK, PT_BANK, Y_BANK, MISC = 0, (2, 5), 3, 4, 6, 7

        def turned(s):
            if s == SCORES:
                return (s - TURNED, s)
            return (s - TURNED,) if TURNED <= s < NU + TURNED and s != SCORES + TURNED else ()

        def w_bank(k):
            return W_BANKS[k % 2]

        def quad(n):
            return 2 * (n // 8) + n % 2, (n % 8) // 2

        def up_bank(u):
            return 0 if u % 2 else 2

        def expert(m, e):
            return 2 * e + m - 1

        block = ctx.enter_context(nc.Block())

        @block.sync
        def _(sp):
            for h in range(2):
                sp.dma_start(xs[:, h * GB:(h + 1) * GB, :],
                             x[h * GB:(h + 1) * GB, :, :].rearrange("b t c -> t b c")).then_inc(ld[f"x{h}"], 16)
            sp.dma_start(ctxT_s, ctxT).then_inc(ld["ctx"], 16)
            sp.dma_start(Wk_s, Wk).then_inc(ld["Wk"], 16)
            sp.dma_start(ident[:, :], consts[:, 0:128]).then_inc(ld["ident"], 16)
            sp.dma_start(wqkvb_s, w_qkvb).then_inc(ld["wqkvb"], 16)
            sp.dma_start(same_head[:, :], consts[:, 128:256]).then_inc(ld["same"], 16)
            sp.dma_start(sel.rearrange("p a b -> p (a b)"), consts[:, 256:256 + DH * 128]).then_inc(ld["sel"], 16)
            sp.dma_start(rows_s[:, :, :].rearrange("p a c -> p (a c)"),
                         rows.rearrange("a c -> (a c)").partition_broadcast(128)).then_inc(ld["rows"], 16)
            sp.dma_start(WrT_s[:, :, :], WrT).then_inc(ld["Wr"], 16)
            sp.dma_start(WvT_s, WvT).then_inc(ld["Wv"], 16)
            sp.dma_start(Wo_s[:, :, :], Wo).then_inc(ld["Wo"], 16)
            sp.dma_start(wout_s, w_out).then_inc(ld["wout"], 16)
            sp.dma_start(mask_s[:, :, :], mask).then_inc(ld["mask"], 16)
            sp.dma_start(Wq_s[:, :], Wq).then_inc(ld["Wq"], 16)
            sp.dma_start(turn_s[:, :], rot_tab).then_inc(ld["tail"], 16)
            sp.dma_start(hw_s[:, :], head_w).then_inc(ld["tail"], 16)
            sp.dma_start(Wg_s[:, :], Wg).then_inc(ld["tail"], 16)
            sp.wait_ge(x2_ps, NG)
            sp.wait_ge(ctxp_ev, len(CTX_UNITS))
            sp.dma_start(W1_s, W1).then_inc(ld["moe"], 16)
            sp.dma_start(W2_s, W2).then_inc(ld["moe"], 16)
            sp.wait_ge(s_ps, XH)
            sp.dma_start(W3_s, W3).then_inc(ld["moe"], 16)
            for b in range(B):
                sp.wait_ge(down_used, 3 * (b + 1))
                sp.dma_start(out[b, :, :], xs[:, b, :]).then_inc(stored, 16)
            sp.wait_ge(stored, 16 * B)

        @block.gpsimd
        def _(pool):
            nc.gpsimd.memset(neg_half[:, :], -0.5).then_inc(pool_own, 1)
            pool.wait_ge(pool_own, 1)

            def inverse_roots(i, g):
                pool.wait_ge(var_ready, i + 1)
                nc.gpsimd.tensor_tensor(rs[:, g * GB:(g + 1) * GB], var[:, g * GB:(g + 1) * GB],
                                        neg_half[:, 0:GB], ALU.pow).then_inc(rs_ready, 1)

            for i in range(4):
                inverse_roots(i, i % 2)
            pool.wait_ge(xn_ready, B)
            nc.gpsimd.tensor_tensor(xs[:, :, :], xs[:, :, :], xn, ALU.add).then_inc(pool_own, 1)
            pool.wait_ge(pool_own, 2)
            pool.wait_ge(z_ready, B)
            pool.wait_ge(kT_ready, 2)
            kv = kT.rearrange("p (b t) -> p b t", b=B)
            kkv = kk.rearrange("p (b t) -> p b t", b=B)
            nc.gpsimd.memset(kkv[:, :, T - 1:T], 0.0).then_inc(kk_ready, 1)
            nc.gpsimd.tensor_tensor(kkv[:, :, 0:T - 1], kv[:, :, 0:T - 1], kv[:, :, 1:T],
                                    ALU.mult).then_inc(kk_ready, 1)
            pool.wait_ge(ld["rows"], 16)
            nc.gpsimd.tensor_tensor(xs[:, :, :], xs[:, :, :],
                                    rows_s[:, 0:1, :].to_broadcast([128, B, C]), ALU.add).then_inc(base_ready, 1)
            pool.wait_ge(ld["mask"], 16)
            nc.gpsimd.tensor_scalar(maskadd[:, :, :], mask_s[:, :, :], NEG, None, ALU.mult).then_inc(mask_ready, 1)
            for i in range(4, 6):
                inverse_roots(i, i % 2)
            for k in range(1, NU):
                pool.wait_ge(w_sines, k + 1)
                pool.wait_ge(w_cosines, k + 1)
                nc.gpsimd.tensor_tensor(wrot[:, k % 4, :], wrot[:, k % 4, :], wsw[:, k % 2, :],
                                        ALU.add).then_inc(w_ready, 1)
                for stage in POST_AT.get(k, ()):
                    if stage in (2, 9):
                        inverse_roots(6 + stage // 9, 0)
            for i in range(8, 10):
                inverse_roots(i, 1)

        @block.scalar
        def _(act):
            act.dma_start(cols_s[:, :], cols).then_inc(ld["cols"], 16)

            def ctx_out(i):
                kind, a, h = CTX_UNITS[i]
                act.wait_ge(ctxp_ps, i + 1)
                if kind == "k":
                    nc.scalar.activation(hk[:, a, h, :, :],
                                         ps[:, 4 + i % 3, 0:GB * J].rearrange("p (b j) -> p b j", b=GB),
                                         ACT.Copy).then_inc(ctxp_ev, 1)
                elif kind == "vo":
                    nc.scalar.activation(VO[:, h, :], ps[:, 4 + i % 3, :], ACT.Copy).then_inc(ctxp_ev, 1)
                else:
                    nc.scalar.activation(hvo[:, a, h, :], ps[0:J, 4 + i % 3, :], ACT.Copy).then_inc(ctxp_ev, 1)

            def ctx_part_out(part):
                for i in range(CTX_PARTS[part - 1], CTX_PARTS[part]):
                    ctx_out(i)

            act.wait_ge(zero_ready, 1)
            nc.scalar.activation(upd[:, 0, 0:1], terms[:, 0, 0, 0:1], ACT.Sqrt).then_inc(table_ready, 1)
            for i in range(CTX_PARTS[0]):
                ctx_out(i)
            act.wait_ge(ld["cols"], 16)
            for h in range(2):
                act.wait_ge(zT_ps, h + 1)
                nc.scalar.activation(nT[:, h * GT:(h + 1) * GT], ps[:, h, :], ACT.Identity,
                                     scale=cols_s[:, 0:1], bias=cols_s[:, 1:2]).then_inc(nT_ready, 1)
            for h in range(2):
                act.wait_ge(k_ps, h + 1)
                nc.scalar.activation(sq[:, h * GT:(h + 1) * GT], ps[:, 2 + h, :], ACT.Square,
                                     bias=cols_s[:, 3:4]).then_inc(sq_ready, 1)
            for h in range(2):
                nc.scalar.activation(kT[:, h * GT:(h + 1) * GT], ps[:, 2 + h, :], ACT.Identity,
                                     bias=cols_s[:, 3:4]).then_inc(kT_ready, 1)
            act.wait_ge(norm_ps, 1)
            nc.scalar.activation(inv[:, :], ps[:, 4, 0:B * NH], ACT.Sqrt).then_inc(norm_ready, 1)

            def spread_out(dst, c, u):
                act.wait_ge(spread_ps, 4 * c + u + 1)
                j = 4 * (u % 2)
                return nc.scalar.activation(
                    dst[:, c % 2, :, :, j:j + 4].rearrange("p t b j -> p j b t"),
                    ps[:, u, :].rearrange("p (j b t) -> p j b t", j=4, b=B), ACT.Copy).then_inc(spread_ev, 1)

            def last_column(dst, src, c):
                return nc.scalar.activation(dst[:, c % 2, :, :, DH].rearrange("p t b -> p b t"),
                                            src.rearrange("p (b t) -> p b t", b=B)[:, :, c * CH:(c + 1) * CH],
                                            ACT.Copy)

            def chunk_out(c):
                if c >= 2:
                    act.wait_ge(scan_done, c - 1)
                spread_out(kx, c, 0)
                spread_out(kx, c, 1)
                last_column(kx, gT, c)
                last_column(mx, vT, c).then_inc(kx_ready, 1)
                if c >= 2:
                    act.wait_ge(att_ps, c - 1)
                spread_out(qx, c, 2)
                spread_out(qx, c, 3)

            def att_out(c):
                act.wait_ge(att_ps, c + 1)
                nc.scalar.activation(attT.rearrange("p (b t) -> p b t", b=B)[:, :, c * CH:(c + 1) * CH],
                                     ps[:, 7, (c % 2) * B * CH:(c % 2 + 1) * B * CH]
                                     .rearrange("p (b t) -> p b t", b=B), ACT.Copy).then_inc(att_ev, 1)

            act.wait_ge(small_ready, 1)
            for h in range(2):
                act.wait_ge(beta_ps, h + 1)
                nc.scalar.activation(beta[:, h * GT:(h + 1) * GT], ps[:, 6 + h, :], ACT.Tanh,
                                     bias=small[:, 0:1], scale=0.5).then_inc(beta_ready, 1)
            spread_out(kx, 0, 0)
            spread_out(kx, 0, 1)
            for h in range(2):
                act.wait_ge(v_ps, h + 1)
                nc.scalar.activation(vT[:, h * GT:(h + 1) * GT], ps[:, 2 + h, :], ACT.Identity,
                                     bias=cols_s[:, 4:5]).then_inc(v_ready, 1)
            act.wait_ge(values_ready, 1)
            last_column(mx, vT, 0).then_inc(first_values, 1)
            act.wait_ge(share_ready, 3)
            last_column(kx, gT, 0).then_inc(kx_ready, 1)
            for h in range(2):
                act.wait_ge(q_ps, h + 1)
                nc.scalar.activation(qT[:, h * GT:(h + 1) * GT], ps[:, 6 + h, :], ACT.Identity,
                                     bias=cols_s[:, 2:3]).then_inc(q_ready, 1)
            spread_out(qx, 0, 2)
            spread_out(qx, 0, 3)
            chunk_out(1)
            ctx_part_out(1)
            for c in range(NC - 2):
                att_out(c)
                chunk_out(c + 2)
                if c == REL_BIAS_AT:
                    act.wait_ge(relb_ps, 1)
                    for r in range(2):
                        nc.scalar.activation(relb[:, r:XH:2], ps[:, 6 + r, r:XH:2], ACT.Copy).then_inc(relb_ready, 1)
                ctx_part_out(c + 2)
            att_out(NC - 2)
            ctx_part_out(NC)
            ctx_part_out(NC + 1)
            att_out(NC - 1)
            ctx_part_out(NC + 2)

            def queries_out(g):
                act.wait_ge(qnT_ps, g + 1)
                nc.scalar.activation(qT[:, g * GT:(g + 1) * GT], ps[:, MISC if g else W_BANKS[0], :],
                                     ACT.Copy).then_inc(qT_ready, 1)

            def hq_out(pair):
                act.wait_ge(hq_ps, pair + 1)
                if pair >= 4:
                    act.wait_ge(s_ps, 2 * (pair - 4) + 2)
                nc.scalar.activation(hqu[:, pair % 4, :], ps[:, HQ_BANK, :], ACT.Identity,
                                     scale=SCALE, bias=small[:, 1:2]).then_inc(hq_ev, 1)

            def swap(k):
                n = k % XH
                act.wait_ge(w_ps, k + 1)
                if k >= 2:
                    act.wait_ge(w_ready, k - 1)
                for r in (0, 64):
                    ins = nc.scalar.activation(wsw[r:r + 64, k % 2, :], ps[64 - r:128 - r, w_bank(k), :],
                                               ACT.Identity, bias=relb[64 - r:128 - r, n:n + 1])
                ins.then_inc(w_swapped, 1)

            def gates_out(g):
                b0, b1 = g * GB, (g + 1) * GB
                act.wait_ge(gate_ps, g + 1)
                nc.scalar.activation(gate[:, b0:b1, :], ps[:, MISC, b0 * XH:b1 * XH]
                                     .rearrange("p (b n) -> p b n", b=GB), ACT.Tanh, scale=0.5).then_inc(gate_t, 1)

            def exponentials(k):
                act.wait_ge(max_ready, k + 1)
                if k >= 4:
                    act.wait_ge(pT_ps, k - 3)
                for b in range(GB):
                    c = GB * k + b
                    ins = nc.scalar.activation(pbuf[:, k % 4, b, :], ps[:, S_BANK + k % 2, b * J:(b + 1) * J],
                                               ACT.Exp, bias=nmax[:, c:c + 1], accum_out=rsum[:, c:c + 1])
                ins.then_inc(p_ready, 1)

            def z3_out(g):
                act.wait_ge(z3T_ps, g + 1)
                nc.scalar.activation(qT[:, g * GT:(g + 1) * GT], ps[:, MISC, :], ACT.Copy).then_inc(z3T_ready, 1)

            def gate_act(g, i):
                u = g * HCH + i
                act.wait_ge(up_ps, u + 1)
                if u >= 3:
                    act.wait_ge(hid_ready, u - 2)
                nc.scalar.activation(gact[:, u % 3, :], ps[:, up_bank(u), :], ACT.Silu).then_inc(act_ready, 1)

            def route_exponentials(g):
                act.wait_ge(route_sub, g + 1)
                nc.scalar.activation(rt[:, 2, :, :], rt[:, 1, :, :], ACT.Exp).then_inc(route_exp, 1)

            nc.scalar.activation(ident_b[:, :], ident[:, :], ACT.Copy).then_inc(identb_ready, 1)
            queries_out(0)
            hq_out(0)
            queries_out(1)
            for s in range(STEPS):
                if s < NU:
                    swap(s)
                if SCORES <= s < NU + SCORES:
                    exponentials(s - SCORES)
                if s in GATES_AT:
                    gates_out(GATES_AT.index(s))
                if s % 2 == 0 and s // 2 + 1 < NP:
                    hq_out(s // 2 + 1)
                if s == Z3_AT:
                    z3_out(0)
                if s == ROUTE_AT + 2:
                    route_exponentials(0)
                if s >= UP_FROM:
                    gate_act(0, s - UP_FROM)

            for i in range(UP_EARLY, HCH):
                gate_act(0, i)
            z3_out(1)
            route_exponentials(1)
            for i in range(HCH):
                gate_act(1, i)

        @block.vector
        def _(dve):
            count = [0]
            norms = [0]

            def own(ins):
                ins.then_inc(vec, 1)
                count[0] += 1

            def settle():
                dve.wait_ge(vec, count[0])

            def stats(src, b0, b1):
                for b in range(b0, b1):
                    own(nc.vector.bn_stats(st[:, b, :], src[:, b, :]))

            def aggregate(b0, b1):
                settle()
                for b in range(b0, b1):
                    own(nc.vector.bn_aggr(mv[:, b, :], st[:, b, :]))

            def variance(b0, b1):
                settle()
                nc.vector.tensor_scalar(var[:, b0:b1], mv[:, b0:b1, 1], LN_EPS, None, ALU.add).then_inc(var_ready, 1)
                norms[0] += 1

            def normalise(dst, src, b0, b1, n, ready=None):
                dve.wait_ge(rs_ready, n)
                for b in range(b0, b1):
                    ins = nc.vector.tensor_scalar(dst[:, b, :], src[:, b, :], mv[:, b, 0:1], rs[:, b:b + 1],
                                                  ALU.subtract, ALU.mult)
                    if ready is None:
                        own(ins)
                    else:
                        ins.then_inc(ready, 1)

            own(nc.vector.memset(hist[:, :, :, :], 0.0))
            nc.vector.memset(terms[:, :, :, :], 0.0).then_inc(zero_ready, 1)
            settle()
            dve.wait_ge(zero_ready, 1)
            own(nc.vector.memset(hist[:, :, :, DH], 1.0))
            for h in range(2):
                dve.wait_ge(ld[f"x{h}"], 16)
                stats(xs, h * GB, (h + 1) * GB)
                aggregate(h * GB, (h + 1) * GB)
                variance(h * GB, (h + 1) * GB)
            dve.wait_ge(ld["cols"], 16)
            nc.vector.tensor_scalar(small[:, 0:1], cols_s[:, 5:6], 0.5, None, ALU.mult)
            own(nc.vector.tensor_scalar(small[:, 1:2], cols_s[:, 6:7], SCALE, None, ALU.mult))
            own(nc.vector.tensor_tensor(small[:, 2:3], cols_s[:, 7:8], cols_s[:, 6:7], ALU.subtract))
            for h in range(2):
                normalise(xn, xs, h * GB, (h + 1) * GB, h + 1, xn_ready)
                dve.wait_ge(xn_ready, (h + 1) * GB)
                stats(xn, h * GB, (h + 1) * GB)
                aggregate(h * GB, (h + 1) * GB)
                variance(h * GB, (h + 1) * GB)
            nc.vector.tensor_scalar(small[:, 3:4], small[:, 2:3], SCALE, None, ALU.mult).then_inc(small_ready, 1)
            for h in range(2):
                normalise(z, xn, h * GB, (h + 1) * GB, h + 3, z_ready)

            dve.wait_ge(norm_ready, 1)
            own(nc.vector.tensor_scalar(inv[:, :], inv[:, :], NORM_EPS, None, ALU.max))
            settle()
            own(nc.vector.reciprocal(inv[:, :], inv[:, :]))
            settle()
            for h in range(2):
                nc.vector.tensor_copy(inv_x[:, h * GT:(h + 1) * GT].rearrange("p (n j) -> p n j", j=DH),
                                      inv[:, h * GB * NH:(h + 1) * GB * NH].unsqueeze(2)
                                      .to_broadcast([128, GB * NH, DH])).then_inc(inv_spread, 1)
            dve.wait_ge(beta_ready, 2)
            dve.wait_ge(inv_ps, 1)
            r = ps[:, 4:6, :].rearrange("p a n -> p (a n)")
            own(nc.vector.scalar_tensor_tensor(beta, beta, 1.0, r, ALU.add, ALU.mult))
            settle()
            nc.vector.scalar_tensor_tensor(fT[:, :], beta, -0.5, r, ALU.mult, ALU.mult).then_inc(inv_used, 1)
            dve.wait_ge(inv_used, 1)
            dve.wait_ge(v_ready, 2)
            nc.vector.scalar_tensor_tensor(vT, beta, 0.5, vT, ALU.mult, ALU.mult).then_inc(values_ready, 1)
            fv = fT[:, :].rearrange("p (b t) -> p b t", b=B)
            gv = gT.rearrange("p (b t) -> p b t", b=B)
            dve.wait_ge(kk_ps, 2)
            nc.vector.memset(gv[:, :, T - 1:T], 0.0).then_inc(share_ready, 1)
            for h in range(2):
                nc.vector.tensor_tensor(gv[:, h * GB:(h + 1) * GB, 0:T - 1],
                                        ps[:, 6 + h, :].rearrange("p (b t) -> p b t", b=GB)[:, :, 0:T - 1],
                                        fv[:, h * GB:(h + 1) * GB, 1:T], ALU.mult).then_inc(share_ready, 1)

            def reads(t):
                c, s = t // CH, t % CH
                if t < 2:
                    dve.wait_ge(spread_ev, 2)
                else:
                    dve.wait_ge(kx_ready, c + 1)
                ft = fT[:, :].rearrange("p (b t) -> p t b", b=B)[:, t, :]
                return nc.vector.tensor_tensor(mx[:, c % 2, s, :, 0:DH], kx[:, c % 2, s, :, 0:DH],
                                               ft.unsqueeze(2).to_broadcast([128, B, DH]), ALU.mult)

            def read_state(t, prev):
                return nc.vector.tensor_tensor(terms[:, (t - 1) % 2, :, DH + 1:], hist[:, prev % CH, :, :],
                                               mx[:, (t // CH) % 2, t % CH, :, :], ALU.mult)

            def update(t):
                return nc.vector.tensor_reduce(upd[:, t % 2, :], terms[:, (t - 1) % 2, :, DH:], AX, ALU.add)

            def attend(c, s0, s1):
                nc.vector.tensor_tensor(qx[:, c % 2, s0:s1, :, :], hist[:, s0:s1, :, 0:DH], qx[:, c % 2, s0:s1, :, :],
                                        ALU.mult).then_inc(scan_done, 1)

            own(reads(0))
            own(reads(1))
            settle()
            dve.wait_ge(first_values, 1)
            own(read_state(0, -1))
            settle()
            dve.wait_ge(table_ready, 1)
            update(0).then_inc(scan_step, 1)
            for t in range(T):
                c, s = t // CH, t % CH
                done = SCAN_OPS * t + 1 - (1 if t == T - 1 else 0)
                if t + 2 < T:
                    reads(t + 2).then_inc(scan_step, 1)
                dve.wait_ge(scan_step, done)
                n = done + (1 if t + 2 < T else 0)
                nc.vector.tensor_tensor(terms[:, t % 2, :, 0:DH + 1], kx[:, c % 2, s, :, :],
                                        upd[:, t % 2, :].unsqueeze(2).to_broadcast([128, B, DH + 1]),
                                        ALU.mult).then_inc(scan_step, 1)
                if t < T - 1:
                    read_state(t + 1, t - 1).then_inc(scan_step, 1)
                dve.wait_ge(scan_step, n + 1)
                nc.vector.tensor_tensor(hist[:, t % CH, :, 0:DH], hist[:, (t - 1) % CH, :, 0:DH],
                                        terms[:, t % 2, :, 0:DH], ALU.add).then_inc(scan_step, 1)
                if t < T - 1:
                    dve.wait_ge(scan_step, n + 2)
                    update(t + 1).then_inc(scan_step, 1)
                if t == T - 1 - TAIL:
                    dve.wait_ge(scan_step, n + 3)
                    dve.wait_ge(spread_ev, 4 * c + 4)
                    attend(c, 0, CH - TAIL)
                elif t == T - 1:
                    dve.wait_ge(scan_step, n + 2)
                    attend(c, CH - TAIL, CH)
                elif s == CH - 1:
                    dve.wait_ge(scan_step, n + 3)
                    dve.wait_ge(spread_ev, 4 * c + 4)
                    attend(c, 0, CH)

            dve.wait_ge(base_ready, 1)
            for g in range(NG):
                b0, b1 = g * GB, (g + 1) * GB
                dve.wait_ge(x2_ps, g + 1)
                own(nc.vector.tensor_tensor(xs[:, b0:b1, :], xs[:, b0:b1, :],
                                            ps[:, g, :].rearrange("p (b c) -> p b c", b=GB), ALU.add))
                settle()
                stats(xs, b0, b1)
                if g == 0:
                    aggregate(b0, b1)
                    variance(b0, b1)
            normalise(qn, xs, 0, GB, 5, qn_ready)
            aggregate(GB, B)
            variance(GB, B)
            normalise(qn, xs, GB, B, 6, qn_ready)

            def maximum(k):
                dve.wait_ge(s_ps, k + 1)
                nc.vector.tensor_reduce(nmax[:, GB * k:GB * k + GB],
                                        ps[:, S_BANK + k % 2, 0:GB * J].rearrange("p (b j) -> p b j", b=GB),
                                        AX, ALU.max, negate=True).then_inc(max_ready, 1)

            def denominators(k):
                dve.wait_ge(p_ready, k + 1)
                own(nc.vector.reciprocal(rden[:, k % 2, :], rsum[:, GB * k:GB * k + GB]))

            def gate_over_denominator(k):
                g, n = k // XH, k % XH
                settle()
                own(nc.vector.tensor_tensor(rden[:, k % 2, :], rden[:, k % 2, :],
                                            gate[:, g * GB:(g + 1) * GB, n], ALU.mult))

            def scale_rows(k):
                settle()
                nc.vector.tensor_tensor(pbuf[:, k % 4, :, :], pbuf[:, k % 4, :, :],
                                        rden[:, k % 2, :].unsqueeze(2).to_broadcast([128, GB, J]),
                                        ALU.mult).then_inc(p_scaled, 1)

            def table(i):
                return turn_s[:, i * T:(i + 1) * T].unsqueeze(1).to_broadcast([128, GB, T])

            def sines(k):
                n = k % XH
                dve.wait_ge(w_swapped, k + 1)
                if k >= 4:
                    dve.wait_ge(s_ps, k - 3)
                nc.vector.scalar_tensor_tensor(wrot[:, k % 4, :].rearrange("p (b i) -> p b i", b=GB),
                                               ps[:, w_bank(k), :].rearrange("p (b i) -> p b i", b=GB),
                                               relb[:, n:n + 1], table(0), ALU.add, ALU.mult).then_inc(w_sines, 1)

            def cosines(k):
                v = wsw[:, k % 2, :].rearrange("p (b i) -> p b i", b=GB)
                nc.vector.tensor_tensor(v, v, table(1), ALU.mult).then_inc(w_cosines, 1)

            def turned_out(k):
                dve.wait_ge(pT_ps, k + 1)
                if k >= 4:
                    dve.wait_ge(y_ps, k - 3)
                nc.vector.tensor_copy(pT[:, k % 4, :, :], ps[0:J, PT_BANK, :].rearrange("p (b i) -> p b i", b=GB)
                                      ).then_inc(pT_ready, 1)

            def post(g, stage):
                b0, b1 = g * GB, (g + 1) * GB
                if stage == 0:
                    dve.wait_ge(y_ready, g + 1)
                    stats(qn, b0, b1)
                elif stage == 1:
                    aggregate(b0, b1)
                elif stage == 2:
                    variance(b0, b1)
                elif stage == 3:
                    normalise(qn, qn, b0, b1, 7 + 2 * g)
                elif stage == 4:
                    settle()
                    own(nc.vector.tensor_tensor(qn[:, b0:b1, :], qn[:, b0:b1, :],
                                                rows_s[:, 1:2, :].to_broadcast([128, GB, C]), ALU.mult))
                elif stage == 5:
                    settle()
                    own(nc.vector.tensor_tensor(qn[:, b0:b1, :], qn[:, b0:b1, :],
                                                rows_s[:, 2:3, :].to_broadcast([128, GB, C]), ALU.add))
                elif stage == 6:
                    settle()
                    own(nc.vector.tensor_tensor(xs[:, b0:b1, :], xs[:, b0:b1, :], qn[:, b0:b1, :], ALU.add))
                elif stage == 7:
                    settle()
                    stats(xs, b0, b1)
                elif stage == 8:
                    aggregate(b0, b1)
                elif stage == 9:
                    variance(b0, b1)
                else:
                    normalise(qn, xs, b0, b1, 8 + 2 * g, z3_ready)
            POST = 11

            def logits(g):
                dve.wait_ge(route_ps, g + 1)
                nc.vector.tensor_copy(rt[:, 0, :, :], ps[:, MISC, 0:GB * EXP].rearrange("p (b e) -> p b e", b=GB)
                                      ).then_inc(logits_ready, 1)

            def route(g, stage):
                logit = rt[:, 0, :, :]
                top1 = rt[:, 3, :, 0:1].to_broadcast([128, GB, EXP])
                top2 = rt[:, 3, :, 1:2].to_broadcast([128, GB, EXP])
                settle()
                if stage == 0:
                    dve.wait_ge(logits_ready, g + 1)
                    for b in range(GB):
                        own(nc.vector.max(rt[:, 3, b, :], rt[:, 0, b, :]))
                elif stage == 1:
                    nc.vector.tensor_tensor(rt[:, 1, :, :], logit, top1, ALU.subtract).then_inc(route_sub, 1)
                    own(nc.vector.tensor_tensor(rt[:, 4, :, :], logit, top2, ALU.is_gt))
                    own(nc.vector.tensor_tensor(rt[:, 5, :, :], logit, top2, ALU.is_equal))
                elif stage == 2:
                    own(nc.vector.tensor_reduce(rt[:, 8, :, 0], rt[:, 4, :, :], AX, ALU.add))
                    own(nc.vector.tensor_copy(rt[:, 6, :, :], rt[:, 5, :, :]))
                elif stage in (3, 4, 5):
                    d = 1 << (stage - 3)
                    a, b_ = (6, 7) if stage != 4 else (7, 6)
                    own(nc.vector.tensor_copy(rt[:, b_, :, 0:d], rt[:, a, :, 0:d]))
                    own(nc.vector.tensor_tensor(rt[:, b_, :, d:EXP], rt[:, a, :, d:EXP],
                                                rt[:, a, :, 0:EXP - d], ALU.add))
                elif stage == 6:
                    own(nc.vector.tensor_tensor(rt[:, 6, :, :], rt[:, 7, :, :],
                                                rt[:, 8, :, 0:1].to_broadcast([128, GB, EXP]), ALU.add))
                elif stage == 7:
                    own(nc.vector.scalar_tensor_tensor(rt[:, 7, :, :], rt[:, 6, :, :], 2.0, rt[:, 5, :, :],
                                                       ALU.is_le, ALU.mult))
                elif stage == 8:
                    own(nc.vector.tensor_tensor(rt[:, 4, :, :], rt[:, 4, :, :], rt[:, 7, :, :], ALU.add))
                elif stage == 9:
                    dve.wait_ge(route_exp, g + 1)
                    own(nc.vector.tensor_tensor(rt[:, 9, :, :], rt[:, 2, :, :], rt[:, 4, :, :], ALU.mult))
                elif stage == 10:
                    own(nc.vector.tensor_reduce(rt[:, 10, :, 0], rt[:, 9, :, :], AX, ALU.add))
                elif stage == 11:
                    own(nc.vector.reciprocal(rt[:, 11, :, 0], rt[:, 10, :, 0]))
                elif stage == 12:
                    own(nc.vector.tensor_tensor(pw[:, g * GB:(g + 1) * GB, :], rt[:, 9, :, :],
                                                rt[:, 11, :, 0:1].to_broadcast([128, GB, EXP]), ALU.mult))
            ROUTE = 13

            def hidden(g, i):
                u = g * HCH + i
                dve.wait_ge(act_ready, u + 1)
                if i == 0 and g:
                    dve.wait_ge(down_ps, g * GB * 3)
                nc.vector.tensor_tensor(hid(i), gact[:, u % 3, :], ps[:, up_bank(u) + 1, :],
                                        ALU.mult).then_inc(hid_ready, 1)

            def experts_sum(b):
                for part, m in enumerate(DOWN):
                    u = b * 3 + part
                    bank = 4 + u % 3
                    dve.wait_ge(down_ps, u + 1)
                    if part:
                        dve.wait_ge(down_used, u)
                    if m == 0:
                        nc.vector.tensor_tensor(xs[:, b, :], ps[:, bank, 0:C], xs[:, b, :],
                                                ALU.add).then_inc(down_used, 1)
                        continue
                    for e in range(4):
                        ex = expert(m, e)
                        if e:
                            settle()
                        ins = nc.vector.scalar_tensor_tensor(
                            xs[:, b, :], ps[:, bank, e * C:(e + 1) * C], pw[:, b, ex:ex + 1],
                            xs[:, b, :], ALU.mult, ALU.add)
                        if e == 3:
                            ins.then_inc(down_used, 1)
                        else:
                            own(ins)

            def attended(g):
                b0, b1 = g * GB, (g + 1) * GB
                dve.wait_ge(y_ps, (g + 1) * XH)
                nc.vector.tensor_tensor(qn[:, b0:b1, :], qn[:, b0:b1, :],
                                        ps[:, Y_BANK, :].rearrange("p (b c) -> p b c", b=GB),
                                        ALU.add).then_inc(y_ready, 1)

            dve.wait_ge(ld["tail"], 48)
            dve.wait_ge(relb_ready, 2)
            for s in range(STEPS):
                k = s - SCALED
                scaling = 0 <= k < NU
                if scaling and k % XH == 0:
                    g = k // XH
                    dve.wait_ge(gate_t, g + 1)
                    own(nc.vector.tensor_scalar(gate[:, g * GB:(g + 1) * GB, :], gate[:, g * GB:(g + 1) * GB, :],
                                                0.5, 0.5, ALU.mult, ALU.add))
                turn_now = turned(s)
                for unit in turn_now[:1]:
                    sines(unit)
                if scaling:
                    denominators(k)
                if scaling:
                    gate_over_denominator(k)
                for unit in turn_now[:1]:
                    cosines(unit)
                    if unit == 0:
                        dve.wait_ge(w_sines, 1)
                        dve.wait_ge(w_cosines, 1)
                        nc.vector.tensor_tensor(wrot[:, 0, :], wrot[:, 0, :], wsw[:, 0, :],
                                                ALU.add).then_inc(w_ready, 1)
                for unit in turn_now[1:]:
                    sines(unit)
                    cosines(unit)
                if scaling:
                    scale_rows(k)
                if SCORES <= s < NU + SCORES:
                    maximum(s - SCORES)
                if TURN <= s < NU + TURN:
                    turned_out(s - TURN)
                if s == HALF:
                    attended(0)
                for stage in POST_AT.get(s, ()):
                    post(0, stage)
                if s == ROUTE_AT:
                    logits(0)
                for stage in (2 * (s - ROUTE_AT - 1), 2 * (s - ROUTE_AT - 1) + 1):
                    if 0 <= stage < ROUTE:
                        route(0, stage)
                if s >= UP_FROM:
                    hidden(0, s - UP_FROM)
            for stage in range(2 * (STEPS - ROUTE_AT - 1), ROUTE):
                route(0, stage)
            attended(1)

            for i in range(UP_EARLY, HCH):
                hidden(0, i)
                post(1, i - UP_EARLY)
            for stage in range(HCH - UP_EARLY, POST):
                post(1, stage)
            for b in range(GB):
                experts_sum(b)
                if b == 1:
                    logits(1)
                for stage in ROUTE_BESIDE[b]:
                    route(1, stage)
            for i in range(HCH):
                hidden(1, i)
            for b in range(GB, B):
                experts_sum(b)

        @block.tensor
        def _(pe):
            def ctx_project(i):
                kind, a, h = CTX_UNITS[i]
                if i >= 3:
                    pe.wait_ge(ctxp_ev, i - 2)
                bank = 4 + i % 3
                if kind == "k":
                    nc.tensor.matmul(ps[:, bank, 0:GB * J], Wk_s[:, h * 128:(h + 1) * 128],
                                     ctxT_s[:, a * GB:(a + 1) * GB, :], start=True, stop=True).then_inc(ctxp_ps, 1)
                elif kind == "vo":
                    for n in range(XH):
                        q, place = quad(n)
                        if q != h:
                            continue
                        r = 64 * (n % 2)
                        ins = nc.tensor.matmul(ps[:, bank, place * C:(place + 1) * C], WvT_s[r:r + 64, n // 2, :],
                                               Wo_s[r:r + 64, n // 2, :], start=True, stop=True)
                    ins.then_inc(ctxp_ps, 1)
                else:
                    nc.tensor.matmul(ps[0:J, bank, :], ctxT_s[:, a, :], VO[:, h, :],
                                     start=True, stop=True).then_inc(ctxp_ps, 1)

            def ctx_part(part):
                for i in range(CTX_PARTS[part - 1] if part else 0, CTX_PARTS[part]):
                    ctx_project(i)

            pe.wait_ge(ld["ctx"], 16)
            pe.wait_ge(ld["Wk"], 16)
            ctx_part(0)
            pe.wait_ge(ld["ident"], 16)
            for b in range(B):
                pe.wait_ge(z_ready, b + 1)
                ins = nc.tensor.transpose(ps[:, b // GB, (b % GB) * T:(b % GB + 1) * T], z[:, b, :], ident[:, :])
                if b % GB == GB - 1:
                    ins.then_inc(zT_ps, 1)
            pe.wait_ge(ld["wqkvb"], 16)

            def project(m, bank, done):
                for h in range(2):
                    pe.wait_ge(nT_ready, h + 1)
                    nc.tensor.matmul(ps[:, bank + h, :], wqkvb_s[:, m * C:(m + 1) * C], nT[:, h * GT:(h + 1) * GT],
                                     start=True, stop=True).then_inc(done, 1)

            def spread(c, u):
                src = kT if u < 2 else qT[:, :]
                n = B * CH
                for j in range(4):
                    ins = nc.tensor.matmul(
                        ps[:, u, j * n:(j + 1) * n], sel[:, 4 * (u % 2) + j, :],
                        src.rearrange("p (b t) -> p b t", b=B)[:, :, c * CH:(c + 1) * CH],
                        start=True, stop=True)
                ins.then_inc(spread_ps, 1)

            def spread_chunk(c):
                for u in range(4):
                    pe.wait_ge(spread_ev, 4 * c + u - 3)
                    spread(c, u)

            def head_sums(src, ready, bank, done):
                for h in range(2):
                    pe.wait_ge(ready, h + 1)
                    nc.tensor.matmul(ps[:, bank + h, :], same_head[:, :], src[:, h * GT:(h + 1) * GT],
                                     start=True, stop=True).then_inc(done, 1)

            project(1, 2, k_ps)
            project(3, 6, beta_ps)
            pe.wait_ge(ld["same"], 16)
            pe.wait_ge(ctxp_ev, CTX_PARTS[0])
            pe.wait_ge(sq_ready, 2)
            for b in range(B):
                ins = nc.tensor.matmul(ps[:, 4, b * NH:(b + 1) * NH], sq[:, b * T:(b + 1) * T],
                                       same_head[:, :].rearrange("p (h j) -> p h j", j=DH)[:, :, 0],
                                       start=True, stop=True)
            ins.then_inc(norm_ps, 1)
            pe.wait_ge(ld["sel"], 16)
            pe.wait_ge(kT_ready, 2)
            spread(0, 0)
            spread(0, 1)
            pe.wait_ge(norm_ready, 1)
            for b in range(B):
                pe.wait_ge(inv_spread, b // GB + 1)
                ins = nc.tensor.matmul(ps[:, 4 + b // GB, (b % GB) * T:(b % GB + 1) * T],
                                       inv_x[:, b * C:(b + 1) * C],
                                       ident[:, :], start=True, stop=True)
            ins.then_inc(inv_ps, 1)
            project(2, 2, v_ps)
            pe.wait_ge(beta_ready, 2)
            pe.wait_ge(kk_ready, 2)
            head_sums(kk, kk_ready, 6, kk_ps)
            pe.wait_ge(share_ready, 3)
            project(0, 6, q_ps)
            pe.wait_ge(v_ready, 2)
            pe.wait_ge(q_ready, 2)
            spread(0, 2)
            spread(0, 3)

            def attend(c):
                cuts = (0, CH) if c < NC - 1 else (0, CH - TAIL, CH)
                if c >= 1:
                    pe.wait_ge(att_ev, c)
                o = ps[:, 7, (c % 2) * B * CH:(c % 2 + 1) * B * CH].rearrange("p (b t) -> p b t", b=B)
                for part in range(len(cuts) - 1):
                    if part:
                        ctx_part(NC + 1)
                    pe.wait_ge(scan_done, c + 1 + part)
                    t0, t1 = cuts[part], cuts[part + 1]
                    for j in range(DH):
                        ins = nc.tensor.matmul(o[:, :, t0:t1], wout_s,
                                               qx[:, c % 2, t0:t1, :, j].rearrange("p t b -> p b t"),
                                               start=(j == 0), stop=(j == DH - 1))
                ins.then_inc(att_ps, 1)

            spread_chunk(1)
            pe.wait_ge(ld["Wv"], 16)
            pe.wait_ge(ld["wout"], 16)
            pe.wait_ge(inv_used, 1)
            pe.wait_ge(ld["Wo"], 16)
            ctx_part(1)
            for c in range(NC - 2):
                attend(c)
                spread_chunk(c + 2)
                if c == REL_BIAS_AT:
                    pe.wait_ge(ld["Wr"], 16)
                    pe.wait_ge(small_ready, 1)
                    pe.wait_ge(att_ev, c + 1)
                    pe.wait_ge(ctxp_ev, CTX_PARTS[c + 1])
                    for n in range(XH):
                        r = 64 * (n % 2)
                        ins = nc.tensor.matmul(ps[:, 6 + n % 2, n:n + 1], WrT_s[r:r + 64, n // 2, :],
                                               small[r:r + 64, 3:4], start=True, stop=True)
                    ins.then_inc(relb_ps, 1)
                    pe.wait_ge(relb_ready, 2)
                ctx_part(c + 2)
            attend(NC - 2)
            pe.wait_ge(scan_step, SCAN_OPS * CTX_LATE)
            ctx_part(NC)
            attend(NC - 1)
            pe.wait_ge(att_ev, NC)
            pe.wait_ge(spread_ev, 4 * NC)
            for b in range(B):
                ins = nc.tensor.transpose(ps[:, b // GB, (b % GB) * C:(b % GB + 1) * C],
                                          attT[:, b * T:(b + 1) * T], ident[:, :])
                if b % GB == GB - 1:
                    ins.then_inc(x2_ps, 1)

            ctx_part(NC + 2)

            def queries(g):
                for bl in range(GB):
                    pe.wait_ge(qn_ready, g * GB + bl + 1)
                    ins = nc.tensor.transpose(ps[:, MISC if g else W_BANKS[0], bl * T:(bl + 1) * T],
                                              qn[:, g * GB + bl, :], ident[:, :])
                ins.then_inc(qnT_ps, 1)

            def hq_project(pair):
                g, p = pair // PAIRS, pair % PAIRS
                if pair:
                    pe.wait_ge(hq_ev, pair)
                nc.tensor.matmul(ps[:, HQ_BANK, :], Wq_s[:, p * 128:(p + 1) * 128],
                                 qT[:, g * GT:(g + 1) * GT], start=True, stop=True).then_inc(hq_ps, 1)

            def relative(k):
                n, r = k % XH, 64 * (k % 2)
                pe.wait_ge(hq_ev, k // 2 + 1)
                if k >= 2:
                    pe.wait_ge(w_swapped, k - 1)
                    pe.wait_ge(w_sines, k - 1)
                nc.tensor.matmul(ps[:, w_bank(k), :], WrT_s[r:r + 64, n // 2, :], hqu[r:r + 64, (k // 2) % 4, :],
                                 start=True, stop=True).then_inc(w_ps, 1)

            def scores(k):
                g, n, r = k // XH, k % XH, 64 * (k % 2)
                bank = S_BANK + k % 2
                pe.wait_ge(w_ready, k + 1)
                if k >= 2:
                    pe.wait_ge(p_ready, k - 1)
                nc.tensor.matmul(ps[:, bank, 0:GB * J], ident_b[:, :], maskadd[:, g * GB:(g + 1) * GB, :],
                                 start=True, stop=False)
                for bl in range(GB):
                    tok = slice(bl * T, (bl + 1) * T)
                    nc.tensor.matmul(ps[:, bank, bl * J:(bl + 1) * J], wrot[:, k % 4, tok], turn_s[:, 2 * T:],
                                     start=False, stop=False)
                    ins = nc.tensor.matmul(ps[:, bank, bl * J:(bl + 1) * J], hqu[r:r + 64, (k // 2) % 4, tok],
                                           hk[r:r + 64, g, n // 2, bl, :],
                                           start=False, stop=(bl == GB - 1))
                ins.then_inc(s_ps, 1)

            def turn(k):
                pe.wait_ge(p_scaled, k + 1)
                if k:
                    pe.wait_ge(pT_ready, k)
                for bl in range(GB):
                    ins = nc.tensor.transpose(ps[0:J, PT_BANK, bl * T:(bl + 1) * T], pbuf[:, k % 4, bl, :],
                                              ident[:, :])
                ins.then_inc(pT_ps, 1)

            def values(k):
                g, n = k // XH, k % XH
                q, place = quad(n)
                pe.wait_ge(pT_ready, k + 1)
                if g and n == 0:
                    pe.wait_ge(y_ready, g)
                for bl in range(GB):
                    ins = nc.tensor.matmul(ps[:, Y_BANK, bl * C:(bl + 1) * C], pT[:, k % 4, bl, :],
                                           hvo[:, g * GB + bl, q, place * C:(place + 1) * C],
                                           start=(n == 0 and bl == 0), stop=(n == XH - 1 and bl == GB - 1))
                ins.then_inc(y_ps, 1)

            def gates(g):
                if g:
                    pe.wait_ge(gate_t, g)
                for b in range(g * GB, (g + 1) * GB):
                    ins = nc.tensor.matmul(ps[:, MISC, b * XH:(b + 1) * XH], qT[:, b * T:(b + 1) * T], hw_s[:, :],
                                           start=True, stop=True)
                ins.then_inc(gate_ps, 1)

            def turn_z3(g):
                for bl in range(GB):
                    pe.wait_ge(z3_ready, g * GB + bl + 1)
                    ins = nc.tensor.transpose(ps[:, MISC, bl * T:(bl + 1) * T], qn[:, g * GB + bl, :], ident[:, :])
                ins.then_inc(z3T_ps, 1)

            def route(g):
                pe.wait_ge(z3T_ready, g + 1)
                for bl in range(GB):
                    b = g * GB + bl
                    ins = nc.tensor.matmul(ps[:, MISC, bl * EXP:(bl + 1) * EXP], qT[:, b * T:(b + 1) * T], Wg_s[:, :],
                                           start=True, stop=True)
                ins.then_inc(route_ps, 1)

            def up(g, i):
                u = g * HCH + i
                if u >= 2:
                    pe.wait_ge(hid_ready, u - 1)
                if u == 1:
                    pe.wait_ge(p_ready, NU)
                bank = up_bank(u)
                nc.tensor.matmul(ps[:, bank, :], W1_s[:, i, :], qT[:, g * GT:(g + 1) * GT],
                                 start=True, stop=True)
                nc.tensor.matmul(ps[:, bank + 1, :], W2_s[:, i, :], qT[:, g * GT:(g + 1) * GT],
                                 start=True, stop=True).then_inc(up_ps, 1)

            def down(g):
                pe.wait_ge(hid_ready, (g + 1) * HCH - 3)
                for bl in range(GB):
                    if g == 0 and bl == 1:
                        pe.wait_ge(logits_ready, 1)
                        turn_z3(1)
                    if g == 0 and bl == 2:
                        route(1)
                    b = g * GB + bl
                    tok = slice(bl * T, (bl + 1) * T)
                    for part, m in enumerate(DOWN):
                        u = b * 3 + part
                        bank = 4 + u % 3
                        if u >= 3:
                            pe.wait_ge(down_used, u - 2)
                        if m == 0:
                            pe.wait_ge(hid_ready, (g + 1) * HCH)
                            for s in range(3):
                                r = 128 if s < 2 else SHID - 256
                                ins = nc.tensor.matmul(ps[:, bank, 0:C], hid(12 + s)[0:r, tok],
                                                       W3_s[0:r, 12 + s, :], start=(s == 0), stop=(s == 2))
                        else:
                            for e in range(4):
                                ex = expert(m, e)
                                r = 64 * (ex % 2)
                                nc.tensor.matmul(ps[:, bank, e * C:(e + 1) * C], hid(ex)[:, tok],
                                                 W3_s[:, ex, :], start=True, stop=False)
                                ins = nc.tensor.matmul(ps[:, bank, e * C:(e + 1) * C],
                                                       hid(EXP + ex // 2)[r:r + REST, tok],
                                                       W3_s[r:r + REST, EXP + ex // 2, :],
                                                       start=False, stop=True)
                        ins.then_inc(down_ps, 1)

            queries(0)
            pe.wait_ge(ld["Wq"], 16)
            pe.wait_ge(ld["tail"], 48)
            pe.wait_ge(identb_ready, 1)
            pe.wait_ge(mask_ready, 1)
            pe.wait_ge(qT_ready, 1)
            hq_project(0)
            queries(1)
            pe.wait_ge(ctxp_ev, len(CTX_UNITS))
            for s in range(STEPS):
                if s == SCORES:
                    relative(s)
                if SCORES <= s < NU + SCORES:
                    scores(s - SCORES)
                if s < NU and s != SCORES:
                    relative(s)
                if s % 2 == 0 and s // 2 + 1 < NP:
                    hq_project(s // 2 + 1)
                if s in GATES_AT:
                    pe.wait_ge(qT_ready, 2)
                    gates(GATES_AT.index(s))
                if TURN <= s < NU + TURN:
                    turn(s - TURN)
                if VALUES <= s < NU + VALUES:
                    values(s - VALUES)
                if s == Z3_AT:
                    turn_z3(0)
                if s == ROUTE_AT:
                    route(0)
                if s == UP_FROM:
                    pe.wait_ge(ld["moe"], 48)
                    pe.wait_ge(w_swapped, NU)
                    pe.wait_ge(w_sines, NU)
                if s >= UP_FROM:
                    up(0, s - UP_FROM)

            for i in range(UP_EARLY, HCH):
                up(0, i)
            down(0)
            for i in range(HCH):
                up(1, i)
            down(1)


def _layout(i):
    import numpy as np
    a = {k: np.asarray(v) for k, v in i.items()}

    def heads(w):
        return np.ascontiguousarray(w.reshape(C, DK, XH).transpose(0, 2, 1).reshape(C, XH * DK))

    def by_pair(w):
        return np.ascontiguousarray(w.reshape(DK, PAIRS, 2, C).transpose(2, 0, 1, 3).reshape(128, PAIRS, C))

    freq = (1.0 / 10000.0 ** (np.arange(0, C, 2, dtype=np.float32) / np.float32(C))).astype(np.float32)
    ang = freq.astype(np.float64)[:, None] * np.arange(T)[None, :]
    sin, cos = np.sin(ang), np.cos(ang)
    key = 0.1 * C * np.concatenate([cos, sin])[:, :J]
    rot = np.concatenate([np.concatenate([sin, sin]), np.concatenate([cos, -cos]), key], 1).astype(np.float32)
    halves = np.concatenate([np.arange(0, C, 2), np.arange(1, C, 2)])

    p = np.arange(128)
    ident = (p[:, None] == p[None, :]).astype(np.float32)
    same = (p[:, None] // DH == p[None, :] // DH).astype(np.float32)
    sel = np.stack([same * (p[:, None] % DH == j) for j in range(DH)], 1).astype(np.float32)
    consts = np.concatenate([ident, same, sel.reshape(128, DH * 128)], 1)

    def up(w, ws):
        o = np.zeros((C, HCH, 128), np.float32)
        o[:, :EXP] = w[:, :, :128].transpose(1, 0, 2)
        for e in range(EXP):
            r = 64 * (e % 2)
            o[:, EXP + e // 2, r:r + REST] = w[e, :, 128:]
        o[:, 12] = ws[:, 0:128]
        o[:, 13] = ws[:, 128:256]
        o[:, 14, :SHID - 256] = ws[:, 256:]
        return o

    w3 = np.zeros((128, HCH, C), np.float32)
    w3[:, :EXP] = a["L0_ffn_W3"][:, :128].transpose(1, 0, 2)
    for e in range(EXP):
        r = 64 * (e % 2)
        w3[r:r + REST, EXP + e // 2] = a["L0_ffn_W3"][e, 128:]
    w3[:, 12] = a["L0_ffn_Ws3"][0:128]
    w3[:, 13] = a["L0_ffn_Ws3"][128:256]
    w3[:SHID - 256, 14] = a["L0_ffn_Ws3"][256:]

    bq = a["L0_attn_b_qkvb"].reshape(4, C)
    twice = lambda v: np.concatenate([v, v])
    cols = np.stack([a["L0_attn_ln_g"], a["L0_attn_ln_b"], bq[0], bq[1], bq[2], bq[3],
                     twice(a["L0_xattn_ub_w"]), twice(a["L0_xattn_vb_w"])], 1)
    rows = np.stack([a["L0_attn_b_out"], a["L0_xattn_ln_g"], a["L0_xattn_ln_b"]])
    return {
        "x": a["x"],
        "ctxT": np.ascontiguousarray(a["ctx_1024"].transpose(2, 0, 1)),
        "mask": np.ascontiguousarray(a["mask_BxSxS2_bf0"].transpose(1, 0, 2)),
        "w_qkvb": a["L0_attn_w_qkvb"], "w_out": a["L0_attn_w_out"], "cols": cols, "rows": rows,
        "consts": consts,
        "Wq": heads(a["L0_xattn_Wq"]), "Wk": heads(a["L0_xattn_Wk"]), "WvT": by_pair(np.ascontiguousarray(a["L0_xattn_Wv"].T)),
        "WrT": by_pair(np.ascontiguousarray(a["L0_xattn_Wr"][halves].T)),
        "Wo": by_pair(a["L0_xattn_Wo"]), "head_w": a["L0_xattn_head_w"], "rot_tab": rot,
        "Wg": a["L0_ffn_Wg"], "W1": up(a["L0_ffn_W1"], a["L0_ffn_Ws1"]),
        "W2": up(a["L0_ffn_W2"], a["L0_ffn_Ws2"]), "W3": w3,
    }


def kernel(**inputs):
    import numpy as np
    import concourse.bacc as bacc
    from concourse import mybir as mb
    from concourse.bass_utils import run_bass_kernel_spmd

    laid = _layout(inputs)
    nc = bacc.Bacc("TRN2", target_bir_lowering=False, num_devices=1)
    arrays, args = {}, []
    for name, a in laid.items():
        a = np.ascontiguousarray(a)
        arrays[f"in_{name}"] = a
        args.append(nc.dram_tensor(f"in_{name}", a.shape, mb.dt.from_np(a.dtype), kind="ExternalInput").ap())
    args.append(nc.dram_tensor("out", (B, T, C), mb.dt.float32, kind="ExternalOutput").ap())
    layer(nc, *args)
    r = run_bass_kernel_spmd(nc, [arrays], core_ids=[0])
    return r.results[0]["out"]
```
